# Optimizing a Trainium2 kernel written in Bass

```python
import numpy as np
import jax
import jax.numpy as jnp

def _softmax(x, axis=-1):
    return jax.nn.softmax(x, axis=axis)

def _gelu(x):
    return jax.nn.gelu(x, approximate=True)

def _silu(x):
    return jax.nn.silu(x)

def _sigmoid(x):
    return jax.nn.sigmoid(x)

def _layernorm(x, axis=-1, eps=1e-05):
    m = jnp.mean(x, axis=axis, keepdims=True)
    v = jnp.var(x, axis=axis, keepdims=True)
    return (x - m) / jnp.sqrt(v + eps)

def _scatter_add(tgt, idx, src, axis=0):
    return tgt.at[idx].add(src)

def _segment_sum(src, seg, n):
    return jax.ops.segment_sum(src, seg, n)
kernel_name = 'mk_lm_tower_d2_tok_ids512_r4_a4935e'

def setup_inputs(seed: int=0):
    np.random.seed(seed)
    _w = jnp.asarray

    def _rec_inputs():
        import jax
        import jax.numpy as jnp
        _rk = jax.random.key(seed)
        x = jax.random.randint(jax.random.fold_in(_rk, 1), (32, 500), 0, 15000, jnp.int32)
        fside_BS_value = -0.00455523 + 1.00028 * jax.random.normal(jax.random.fold_in(_rk, 21), (32, 500), jnp.float32)
        return (x, fside_BS_value)
    x, fside_BS_value = _rec_inputs()

    def _L0_tok_setup():
        import jax, jax.numpy as jnp
        import numpy as np
        D_TOKEN = 128
        IN_FEATURE = 500
        VOCAB = 15000
        BATCH = 32
        EPS = 1e-05

        def layer_norm(x, gamma, beta):
            mu = jnp.mean(x, axis=-1, keepdims=True)
            var = jnp.mean(jnp.square(x - mu), axis=-1, keepdims=True)
            return (x - mu) * jax.lax.rsqrt(var + EPS) * gamma + beta
        key = jax.random.key(seed)
        ks = jax.random.split(key, 8)
        inv_sqrt_d = 1.0 / np.sqrt(D_TOKEN)
        gene = jax.random.randint(ks[0], (BATCH, IN_FEATURE), 0, VOCAB, dtype=jnp.int64 if jax.config.read('jax_enable_x64') else jnp.int32)
        value = jax.random.normal(ks[1], (BATCH, IN_FEATURE), dtype=jnp.float32)
        emb_table = jax.random.normal(ks[2], (VOCAB, D_TOKEN), dtype=jnp.float32)
        w_val = jax.random.normal(ks[3], (IN_FEATURE, D_TOKEN), dtype=jnp.float32) * inv_sqrt_d
        b_val = jax.random.normal(ks[4], (IN_FEATURE, D_TOKEN), dtype=jnp.float32) * inv_sqrt_d
        gamma_g = jnp.ones((D_TOKEN,), jnp.float32)
        beta_g = jnp.zeros((D_TOKEN,), jnp.float32)
        gamma_v = jnp.ones((D_TOKEN,), jnp.float32)
        beta_v = jnp.zeros((D_TOKEN,), jnp.float32)
        return {'gene': gene, 'value': value, 'emb_table': emb_table, 'w_val': w_val, 'b_val': b_val, 'gamma_g': gamma_g, 'beta_g': beta_g, 'gamma_v': gamma_v, 'beta_v': beta_v}
    _L0_tok_all = _L0_tok_setup()
    _L0_tok_in = {k: v for k, v in _L0_tok_all.items() if k in ('emb_table', 'w_val', 'b_val', 'gamma_g', 'beta_g', 'gamma_v', 'beta_v')}
    del _L0_tok_all

    def _L0_attn_setup():
        import jax, jax.numpy as jnp
        import numpy as np
        B, L, D = (4, 2048, 128)

        def _mingru_scan(gates, cands):
            a = 1.0 - gates
            b = gates * cands

            def combine(left, right):
                a_l, b_l = left
                a_r, b_r = right
                return (a_r * a_l, a_r * b_l + b_r)
            _, h = jax.lax.associative_scan(combine, (a, b), axis=1)
            return h
        key = jax.random.key(seed)
        kx, kwg, kwc = jax.random.split(key, 3)
        x = jax.random.normal(kx, (B, L, D), dtype=jnp.float32)
        bound = float(np.sqrt(6.0 / (D + D)))
        Wg = jax.random.uniform(kwg, (D, D), minval=-bound, maxval=bound, dtype=jnp.float32)
        bg = jnp.ones((D,), dtype=jnp.float32)
        Wc = jax.random.uniform(kwc, (D, D), minval=-bound, maxval=bound, dtype=jnp.float32)
        bc = jnp.zeros((D,), dtype=jnp.float32)
        return {'x': x, 'Wg': Wg, 'bg': bg, 'Wc': Wc, 'bc': bc}
    _L0_attn_all = _L0_attn_setup()
    _L0_attn_in = {k: v for k, v in _L0_attn_all.items() if k in ('Wg', 'bg', 'Wc', 'bc')}
    del _L0_attn_all

    def _L0_ffn_setup():
        import jax, jax.numpy as jnp
        import numpy as np
        E = 64
        K = 2
        D = 128
        H = 64
        NSH = 2
        ROUTE_SCALE = 2.5
        CAP = 256
        STD = 0.02
        key = jax.random.key(seed)
        ks = jax.random.split(key, 8)
        x = jax.random.normal(ks[0], (4, 512, D), dtype=jnp.float32)
        gate_w = jax.random.normal(ks[1], (E, D), dtype=jnp.float32) * STD
        w1 = jax.random.normal(ks[2], (E, D, H), dtype=jnp.float32) * STD
        w3 = jax.random.normal(ks[3], (E, D, H), dtype=jnp.float32) * STD
        w2 = jax.random.normal(ks[4], (E, H, D), dtype=jnp.float32) * STD
        sw1 = jax.random.normal(ks[5], (D, H * NSH), dtype=jnp.float32) * STD
        sw3 = jax.random.normal(ks[6], (D, H * NSH), dtype=jnp.float32) * STD
        sw2 = jax.random.normal(ks[7], (H * NSH, D), dtype=jnp.float32) * STD
        return {'x': x, 'gate_w': gate_w, 'w1': w1, 'w3': w3, 'w2': w2, 'sw1': sw1, 'sw3': sw3, 'sw2': sw2}
    _L0_ffn_all = _L0_ffn_setup()
    _L0_ffn_in = {k: v for k, v in _L0_ffn_all.items() if k in ('gate_w', 'w1', 'w3', 'w2', 'sw1', 'sw3', 'sw2')}
    del _L0_ffn_all

    def _L1_attn_setup():
        import jax, jax.numpy as jnp
        import numpy as np
        NUM_HEADS = 8
        key = jax.random.key(seed)
        k1, k2, k3 = jax.random.split(key, 3)
        B, N, C = (4, 512, 128)
        x = jax.random.normal(k1, (B, N, C), dtype=jnp.float32)
        q_w = jax.random.normal(k2, (C, C), dtype=jnp.float32) * 0.02
        kv_w = jax.random.normal(k3, (2 * C, C), dtype=jnp.float32) * 0.02
        return {'x': x, 'q_w': q_w, 'kv_w': kv_w}
    _L1_attn_all = _L1_attn_setup()
    _L1_attn_in = {k: v for k, v in _L1_attn_all.items() if k in ('q_w', 'kv_w')}
    del _L1_attn_all

    def _L1_ffn_setup():
        import jax, jax.numpy as jnp
        import numpy as np
        MARK_AX, OP_ADD, OP_SUB = (0, 1, 2)
        ALU_LO, ALU_HI = (16, 32)
        AX_CARRY_LO, AX_CARRY_HI = (48, 64)
        OPCODE_BASE = 80
        OUTPUT_LO, OUTPUT_HI, CARRY = (128, 144, 160)
        NIB_A, NIB_B, OP_START = (0, 1, 10)
        RESULT, CARRY_OUT = (100, 101)
        GE_POS, GE_DIM = (8, 160)
        OPC_ADD, OPC_SUB = (25, 26)
        B, S, D = (8, 1024, 128)

        def _decode_nibble(x, base):
            return jnp.argmax(x[..., base:base + 16] > 0.5, axis=-1).astype(x.dtype)

        def _pipeline(h, W, b):
            for i in range(3):
                h = jnp.einsum('bspd,od->bspo', h, W[i]) + b[i]
                if i < 2:
                    h = jax.nn.relu(h)
            return h
        key = jax.random.key(seed)
        kx, k1, k2, k3, k4 = jax.random.split(key, 5)
        x_bd = jax.random.uniform(kx, (B, S, D), dtype=jnp.float32)
        Wa = jax.random.normal(k1, (3, GE_DIM, GE_DIM), dtype=jnp.float32) * 0.05
        ba = jax.random.normal(k2, (3, GE_DIM), dtype=jnp.float32) * 0.05
        Ws = jax.random.normal(k3, (3, GE_DIM, GE_DIM), dtype=jnp.float32) * 0.05
        bs = jax.random.normal(k4, (3, GE_DIM), dtype=jnp.float32) * 0.05
        return {'x_bd': x_bd, 'Wa': Wa, 'ba': ba, 'Ws': Ws, 'bs': bs}
    _L1_ffn_all = _L1_ffn_setup()
    _L1_ffn_in = {k: v for k, v in _L1_ffn_all.items() if k in ('Wa', 'ba', 'Ws', 'bs')}
    del _L1_ffn_all
    return {'x': x, 'fside_BS_value': fside_BS_value, 'L0_tok_emb_table': _L0_tok_in['emb_table'], 'L0_tok_w_val': _L0_tok_in['w_val'], 'L0_tok_b_val': _L0_tok_in['b_val'], 'L0_tok_gamma_g': _L0_tok_in['gamma_g'], 'L0_tok_beta_g': _L0_tok_in['beta_g'], 'L0_tok_gamma_v': _L0_tok_in['gamma_v'], 'L0_tok_beta_v': _L0_tok_in['beta_v'], 'L0_attn_Wg': _L0_attn_in['Wg'], 'L0_attn_bg': _L0_attn_in['bg'], 'L0_attn_Wc': _L0_attn_in['Wc'], 'L0_attn_bc': _L0_attn_in['bc'], 'L0_ffn_gate_w': _L0_ffn_in['gate_w'], 'L0_ffn_w1': _L0_ffn_in['w1'], 'L0_ffn_w3': _L0_ffn_in['w3'], 'L0_ffn_w2': _L0_ffn_in['w2'], 'L0_ffn_sw1': _L0_ffn_in['sw1'], 'L0_ffn_sw3': _L0_ffn_in['sw3'], 'L0_ffn_sw2': _L0_ffn_in['sw2'], 'L1_attn_q_w': _L1_attn_in['q_w'], 'L1_attn_kv_w': _L1_attn_in['kv_w'], 'L1_ffn_Wa': _L1_ffn_in['Wa'], 'L1_ffn_ba': _L1_ffn_in['ba'], 'L1_ffn_Ws': _L1_ffn_in['Ws'], 'L1_ffn_bs': _L1_ffn_in['bs']}

def reference(x, fside_BS_value, L0_tok_emb_table, L0_tok_w_val, L0_tok_b_val, L0_tok_gamma_g, L0_tok_beta_g, L0_tok_gamma_v, L0_tok_beta_v, L0_attn_Wg, L0_attn_bg, L0_attn_Wc, L0_attn_bc, L0_ffn_gate_w, L0_ffn_w1, L0_ffn_w3, L0_ffn_w2, L0_ffn_sw1, L0_ffn_sw3, L0_ffn_sw2, L1_attn_q_w, L1_attn_kv_w, L1_ffn_Wa, L1_ffn_ba, L1_ffn_Ws, L1_ffn_bs):
    import jax
    import jax.numpy as jnp

    def _L0_tok_ref(gene, value, emb_table, w_val, b_val, gamma_g, beta_g, gamma_v, beta_v):
        import jax, jax.numpy as jnp
        import numpy as np
        D_TOKEN = 128
        IN_FEATURE = 500
        VOCAB = 15000
        BATCH = 32
        EPS = 1e-05

        def layer_norm(x, gamma, beta):
            mu = jnp.mean(x, axis=-1, keepdims=True)
            var = jnp.mean(jnp.square(x - mu), axis=-1, keepdims=True)
            return (x - mu) * jax.lax.rsqrt(var + EPS) * gamma + beta
        g = emb_table[gene]
        g = layer_norm(g, gamma_g, beta_g)
        v = w_val[None] * value[..., None] + b_val[None]
        v = layer_norm(v, gamma_v, beta_v)
        return g + v

    def _L0_attn_ref(x, Wg, bg, Wc, bc):
        import jax, jax.numpy as jnp
        import numpy as np
        B, L, D = (4, 2048, 128)

        def _mingru_scan(gates, cands):
            a = 1.0 - gates
            b = gates * cands

            def combine(left, right):
                a_l, b_l = left
                a_r, b_r = right
                return (a_r * a_l, a_r * b_l + b_r)
            _, h = jax.lax.associative_scan(combine, (a, b), axis=1)
            return h
        gates = jax.nn.sigmoid(jnp.einsum('bld,ed->ble', x, Wg) + bg)
        cands = jnp.tanh(jnp.einsum('bld,ed->ble', x, Wc) + bc)
        return _mingru_scan(gates, cands)

    def _L0_ffn_ref(x, gate_w, w1, w3, w2, sw1, sw3, sw2):
        import jax, jax.numpy as jnp
        import numpy as np
        E = 64
        K = 2
        D = 128
        H = 64
        NSH = 2
        ROUTE_SCALE = 2.5
        CAP = 256
        STD = 0.02
        bs, slen, d = x.shape
        xf = x.reshape(-1, d)
        logits = xf @ gate_w.T
        scores = jax.nn.sigmoid(logits.astype(jnp.float32))
        top_scores, top_idx = jax.lax.top_k(scores, K)
        top_scores = top_scores / (top_scores.sum(-1, keepdims=True) + 1e-20)
        top_scores = top_scores * ROUTE_SCALE
        flat_e = top_idx.reshape(-1)
        x_pairs = jnp.repeat(xf, K, axis=0)
        oh = jax.nn.one_hot(flat_e, E, dtype=jnp.int32)
        pos = jnp.take_along_axis(jnp.cumsum(oh, axis=0), flat_e[:, None], axis=1)[:, 0] - 1
        buf = jnp.zeros((E, CAP, d), dtype=xf.dtype).at[flat_e, pos].set(x_pairs, mode='drop')
        h = jax.nn.silu(jnp.einsum('ecd,edh->ech', buf, w1)) * jnp.einsum('ecd,edh->ech', buf, w3)
        y = jnp.einsum('ech,ehd->ecd', h, w2)
        valid = (pos < CAP)[:, None]
        y_pairs = jnp.where(valid, y[flat_e, jnp.minimum(pos, CAP - 1)], 0.0)
        routed = (y_pairs.reshape(-1, K, d) * top_scores[..., None].astype(xf.dtype)).sum(axis=1)
        shared = jax.nn.silu(xf @ sw1) * (xf @ sw3) @ sw2
        return (shared + routed).reshape(bs, slen, d)

    def _L1_attn_ref(x, q_w, kv_w):
        import jax, jax.numpy as jnp
        import numpy as np
        NUM_HEADS = 8
        B, N, C = x.shape
        H = NUM_HEADS
        D = C // H
        halfB = B // 2
        q = (x @ q_w.T).reshape(B, N, H, D)
        kv = (x @ kv_w.T).reshape(B, N, 2, H, D)
        k, v = (kv[:, :, 0], kv[:, :, 1])
        k = jnp.concatenate([k[halfB:], k[:halfB]], axis=0)
        v = jnp.concatenate([v[halfB:], v[:halfB]], axis=0)
        scores = jnp.einsum('bnhd,bmhd->bhnm', q, k) / jnp.sqrt(jnp.float32(C))
        prob = jax.nn.softmax(scores, axis=-1)
        out = jnp.einsum('bhnm,bmhd->bndh', prob, v).reshape(B, N, C)
        return out

    def _L1_ffn_ref(x_bd, Wa, ba, Ws, bs):
        import jax, jax.numpy as jnp
        import numpy as np
        MARK_AX, OP_ADD, OP_SUB = (0, 1, 2)
        ALU_LO, ALU_HI = (16, 32)
        AX_CARRY_LO, AX_CARRY_HI = (48, 64)
        OPCODE_BASE = 80
        OUTPUT_LO, OUTPUT_HI, CARRY = (128, 144, 160)
        NIB_A, NIB_B, OP_START = (0, 1, 10)
        RESULT, CARRY_OUT = (100, 101)
        GE_POS, GE_DIM = (8, 160)
        OPC_ADD, OPC_SUB = (25, 26)
        B, S, D = (8, 1024, 128)

        def _decode_nibble(x, base):
            return jnp.argmax(x[..., base:base + 16] > 0.5, axis=-1).astype(x.dtype)

        def _pipeline(h, W, b):
            for i in range(3):
                h = jnp.einsum('bspd,od->bspo', h, W[i]) + b[i]
                if i < 2:
                    h = jax.nn.relu(h)
            return h
        x = x_bd
        Bsz, seq, _ = x.shape
        x_ge = jnp.zeros((Bsz, seq, GE_POS, GE_DIM), dtype=x.dtype)
        x_ge = x_ge.at[..., 0, NIB_A].set(_decode_nibble(x, ALU_LO))
        x_ge = x_ge.at[..., 1, NIB_A].set(_decode_nibble(x, ALU_HI))
        x_ge = x_ge.at[..., 0, NIB_B].set(_decode_nibble(x, AX_CARRY_LO))
        x_ge = x_ge.at[..., 1, NIB_B].set(_decode_nibble(x, AX_CARRY_HI))
        x_ge = x_ge.at[..., :, OP_START + OPC_ADD].set(x[..., OPCODE_BASE + OPC_ADD][..., None])
        x_ge = x_ge.at[..., :, OP_START + OPC_SUB].set(x[..., OPCODE_BASE + OPC_SUB][..., None])
        mark = x[..., MARK_AX] > 0.5
        m_add = mark & (x[..., OP_ADD] > 0.5)
        m_sub = mark & ~(x[..., OP_ADD] > 0.5) & (x[..., OP_SUB] > 0.5)
        active = (m_add | m_sub).astype(x.dtype)
        y_add = _pipeline(x_ge, Wa, ba)
        y_sub = _pipeline(x_ge, Ws, bs)
        y = jnp.where(m_add[..., None, None], y_add, jnp.where(m_sub[..., None, None], y_sub, x_ge))
        res_lo = jnp.clip(jnp.round(y[..., 0, RESULT]), 0, 15).astype(jnp.int32)
        res_hi = jnp.clip(jnp.round(y[..., 1, RESULT]), 0, 15).astype(jnp.int32)
        oh_lo = jax.nn.one_hot(res_lo, 16, dtype=x.dtype) * active[..., None]
        oh_hi = jax.nn.one_hot(res_hi, 16, dtype=x.dtype) * active[..., None]
        carry = (jnp.round(y[..., 1, CARRY_OUT]) > 0.5).astype(x.dtype) * active
        out = x
        out = out.at[..., OUTPUT_LO:OUTPUT_LO + 16].add(2.0 * oh_lo)
        out = out.at[..., OUTPUT_HI:OUTPUT_HI + 16].add(2.0 * oh_hi)
        out = out.at[..., CARRY].add(carry)
        return out
    h = _L0_tok_ref(x, fside_BS_value, L0_tok_emb_table, L0_tok_w_val, L0_tok_b_val, L0_tok_gamma_g, L0_tok_beta_g, L0_tok_gamma_v, L0_tok_beta_v)
    h = h + _L0_attn_ref(_layernorm(h, axis=-1), L0_attn_Wg, L0_attn_bg, L0_attn_Wc, L0_attn_bc)
    h = h + _L0_ffn_ref(_layernorm(h, axis=-1), L0_ffn_gate_w, L0_ffn_w1, L0_ffn_w3, L0_ffn_w2, L0_ffn_sw1, L0_ffn_sw3, L0_ffn_sw2)
    h = h + _L1_attn_ref(_layernorm(h, axis=-1), L1_attn_q_w, L1_attn_kv_w)
    h = h + _L1_ffn_ref(_layernorm(h, axis=-1), L1_ffn_Wa, L1_ffn_ba, L1_ffn_Ws, L1_ffn_bs)
    return h

_drawn_inputs = setup_inputs


def setup_inputs(seed=0):
    import zlib

    import numpy as np

    out = dict(_drawn_inputs(seed))
    spreads = {'L0_tok_gamma_g': (1.0, 0.2),
     'L0_tok_beta_g': (0.0, 0.1),
     'L0_tok_gamma_v': (1.0, 0.2),
     'L0_tok_beta_v': (0.0, 0.1),
     'L0_attn_bg': (1.0, 0.6),
     'L0_attn_bc': (0.0, 0.1)}
    factors = {'L0_ffn_gate_w': 8.0,
     'L0_ffn_w1': 8.0,
     'L0_ffn_w3': 8.0,
     'L0_ffn_w2': 8.0,
     'L0_ffn_sw1': 8.0,
     'L0_ffn_sw3': 8.0,
     'L0_ffn_sw2': 8.0,
     'L1_attn_q_w': 49.386,
     'L1_attn_kv_w': 13.141}
    for name, (base, spread) in spreads.items():
        noise = np.random.default_rng([zlib.crc32(name.encode()), seed]).standard_normal(out[name].shape)
        drawn = base * np.exp(spread * noise) if base else spread * noise
        out[name] = jnp.asarray(drawn.astype(out[name].dtype))
    for name, factor in factors.items():
        out[name] = (out[name] * factor).astype(out[name].dtype)
    return out
```

```python
from contextlib import ExitStack

import concourse.bass as bass
from concourse import mybir

B, L, D = 32, 500, 128
C, T = 4, 125
NT = B * C
E, CAP, HID = 64, 256, 64
SLOTS = E * CAP
H, DH = 8, 16
EPS = 1e-5
FAR = 65536.0

F32, BF16, I32, U32 = mybir.dt.float32, mybir.dt.bfloat16, mybir.dt.int32, mybir.dt.uint32
ALU = mybir.AluOpType
ACT = mybir.ActivationFunctionType
AX = mybir.AxisListType


class Step:

    def __init__(self, i, reg=None):
        self.q4, self.q2 = i % 4, i % 2
        if reg is None:
            self.first = i
            self.b, self.b2, self.b4 = i, i // 2, i // 4
        else:
            self.first = None
            self.b, self.b2, self.b4 = reg * 4 + i, reg * 2 + i // 2, reg + i // 4

    def tile(self):
        return self.b * C

    def after(self, n):
        return self.first is None or self.first >= n


class Iteration:

    def __init__(self, i, reg=None):
        self.i, self.reg, self.now = i, reg, Step(i, reg)

    def __call__(self, lag):
        if self.reg is None and not 0 <= self.i - lag < B:
            return None
        return Step(self.i - lag, self.reg)


def pipeline(eng, last, body, count=None, loop_from=8, trips=6):
    per = 0
    for i in range(loop_from):
        at = count.n if count else 0
        body(Iteration(i))
        per = count.n - at if count else 0
    if count:
        count.enter(per * 4)
    with eng.Fori(0, trips) as reg:
        if count:
            count.reg = reg
        for k in range(4):
            body(Iteration(loop_from + k, reg))
    if count:
        count.leave(trips)
    for i in range(loop_from + 4 * trips, last + 1):
        body(Iteration(i))


class Count:

    def __init__(self, sem):
        self.sem, self.n, self.reg, self.per = sem, 0, None, 0

    def enter(self, per):
        self.per, self.at_entry = per, self.n

    def leave(self, trips):
        assert self.n - self.at_entry == self.per, (self.n - self.at_entry, self.per)
        self.n = self.at_entry + self.per * trips
        self.reg, self.per = None, 0

    def now(self):
        return self.reg * self.per + self.n if self.reg is not None else self.n

    def done(self, ins):
        ins.then_inc(self.sem, 1)
        self.n += 1
        return self.now()


def wait_apart(eng, set_up, sem, value):
    if not isinstance(value, int):
        value = eng.to_reg(value)
    eng.wait_ge(set_up, 1)
    eng.wait_ge(sem, value)


def bc(ap, axis, n, shape):
    return ap.unsqueeze(axis).to_broadcast(shape)


def build(nc, io, out):
    top = ExitStack()
    with top:
        def sb(name, shape, dt=F32, ctx=top):
            return ctx.enter_context(nc.sbuf_tensor(name, shape, dt))

        def pb(name, shape, dt=F32, ctx=top):
            return ctx.enter_context(nc.psum_tensor(name, shape, dt))

        keep = {
            "h": sb("h", [T, NT, D]),
            "ident": sb("ident", [128, 128]),
            "w_t": sb("w_t", [128, 6, 128]),
            "top_scores": sb("top_scores", [T, NT, 2]),
            "slots": sb("slots", [T, NT, 2]),
        }
        dram = {
            "x_slots": nc.dram_tensor("x_slots", (SLOTS, D), F32, kind="Internal").ap(),
            "y_slots": nc.dram_tensor("y_slots", (SLOTS, D), F32, kind="Internal").ap(),
            "x_t": nc.dram_tensor("x_t", (B, D, L), F32, kind="Internal").ap(),
        }
        front(nc, io, keep, dram)
        experts(nc, io, keep, dram)
        attention(nc, io, keep, dram, out)


def front(nc, io, keep, dram):
    with ExitStack() as ctx:
        def sb(name, shape, dt=F32):
            return ctx.enter_context(nc.sbuf_tensor(name, shape, dt))

        def pb(name, shape, dt=F32):
            return ctx.enter_context(nc.psum_tensor(name, shape, dt))

        def sem(name):
            return ctx.enter_context(nc.semaphore(name))

        h, ident, w_t = keep["h"], keep["ident"], keep["w_t"]
        w_cv = sb("w_cv", [T, C, D])
        b_cv = sb("b_cv", [T, C, D])
        gamma_g = sb("gamma_g", [T, D])
        beta = sb("beta", [T, D])
        v_scale = sb("v_scale", [T, NT])
        v_rstd = sb("v_rstd", [T, NT])
        ids_t = sb("ids_t", [T, NT], I32)
        bias = sb("bias", [128, 2])
        before = sb("before", [T, T], BF16)
        not_before = sb("not_before", [T, T], BF16)
        ones = sb("ones", [T, T], BF16)
        expert_no = sb("expert_no", [T, E])
        zeros = sb("zeros", [128, 2048])
        eps = sb("eps", [128, 1])
        banks = [pb(f"a_bank{k}", [128, 512]) for k in range(8)]

        ids = sb("ids", [T, 4, C], I32)
        g = sb("g", [T, 4, C, D])
        gn = sb("gn", [T, 2, C, D])
        vn = sb("vn", [T, 2, C, D])
        stats = sb("stats", [T, 3, C, 6])
        moments = sb("moments", [T, 2, 3, C, 2])
        std = sb("std", [T, 2, 3, C])
        rstd = sb("rstd", [T, 2, 3, C])
        shift = sb("shift", [T, 2, 3, C])
        xn = sb("xn", [T, 2, C, D])
        xn_t = sb("xn_t", [D, 2, L])
        hold = sb("hold", [D, 2, L])
        cand = sb("cand", [D, 2, L])
        inflow = sb("inflow", [D, 2, L])
        scan = sb("scan", [D, 2, L])
        x3 = sb("x3", [T, 4, C, D])
        x3_t = sb("x3_t", [D, 2, L])
        top8 = sb("top8", [T, 2, C, 8])
        top_i = sb("top_i", [T, 2, C, 8], U32)
        expert = sb("expert", [T, 2, C, 2])
        hot = sb("hot", [T, 2, C, 2, E], BF16)
        mask = sb("mask", [T, 2, C, E], BF16)
        rank_e = sb("rank_e", [T, C, 2, E])
        pos = sb("pos", [T, C, 2])
        late = sb("late", [T, C, 2])
        slot_0 = sb("slot_0", [T, C, 2])
        slot_i = sb("slot_i", [T, 4, C * 2], I32)
        flag = sb("flag", [1, 1])
        no_mask = sb("no_mask", [T, C * E], BF16)
        xt_ps, gate_ps, cand_ps, scan_ps, x3t_ps, logit_ps, rank_ps = banks[:7]

        gathered = [sem(f"gathered{k}") for k in range(4)]
        scattered = [sem(f"scattered{k}") for k in range(4)]
        x_stored = [sem(f"x_stored{k}") for k in range(2)]
        ids_ready = sem("ids_ready")
        zero_filled = sem("zero_filled")
        stats_ready = sem("stats_ready")
        std_ready = sem("std_ready")
        shift_ready = sem("shift_ready")
        normed = sem("normed")
        values_scaled = sem("values_scaled")
        h_summed = sem("h_summed")
        x_ready = sem("x_ready")
        xt_ready = sem("xt_ready")
        xt_copied = sem("xt_copied")
        gates_ready = sem("gates_ready")
        gates_acted = sem("gates_acted")
        scanned = sem("scanned")
        scan_t_ready = sem("scan_t_ready")
        scan_added = sem("scan_added")
        x3_ready = sem("x3_ready")
        x3t_ready = sem("x3t_ready")
        x3t_copied = sem("x3t_copied")
        logits_ready = sem("logits_ready")
        top_ready = sem("top_ready")
        scored = sem("scored")
        masked = sem("masked")
        rank_ready = sem("rank_ready")
        rank_read = sem("rank_read")
        rank_next = sem("rank_next")
        pos_ready = sem("pos_ready")
        slot_ready = sem("slot_ready")
        dve_done = sem("dve_done")
        set_up = sem("set_up")
        fill = dram["x_slots"].rearrange("(n p r) d -> n p (r d)", p=128, r=16)
        setup(nc, io, keep, locals())
        block = ctx.enter_context(nc.Block())

        LAST = B + 5

        @block.sync
        def _(sp):
            def body(it):
                if s := it(5):
                    sp.wait_ge(x3t_copied, s.b + 1)
                    sp.dma_start(dram["x_t"][bass.ds(s.b, 1), :, :].rearrange("a d l -> d (a l)"),
                                 x3_t[:, s.q2, :]).then_inc(x_stored[s.q2], 16)

            sp.wait_ge(gathered[3], 64)
            for n in range(SLOTS // 2048):
                sp.dma_start(fill[n, :, :], zeros[:, :]).then_inc(zero_filled, 16)
            pipeline(sp, LAST, body)
            for k in range(2):
                sp.wait_ge(x_stored[k], 16 * B // 2)

        @block.gpsimd
        def _(pool):
            def gather(s):
                if s.after(4):
                    pool.wait_ge(gathered[s.q4], s.b4 * 64)
                    wait_apart(pool, set_up, normed, s.b - 3)
                pool.tensor_copy(ids[:, s.q4, :], ids_t[:, bass.ds(s.tile(), C)]).then_inc(ids_ready, 1)
                wait_apart(pool, set_up, ids_ready, s.b + 1)
                for c in range(C):
                    pool.indirect_dma_start(
                        out=g[:, s.q4, c, :], out_offset=None, in_=io["L0_tok_emb_table"],
                        in_offset=bass.IndirectOffsetOnAxis(ap=ids[:, s.q4, c:c + 1], axis=0),
                    ).then_inc(gathered[s.q4], 16)

            def scatter(s):
                wait_apart(pool, set_up, slot_ready, s.b + 1)
                for j in range(2 * C):
                    pool.indirect_dma_start(
                        out=dram["x_slots"],
                        out_offset=bass.IndirectOffsetOnAxis(ap=slot_i[:, s.q4, j:j + 1], axis=0),
                        in_=x3[:, s.q4, j // 2, :], in_offset=None,
                        bounds_check=SLOTS - 1, oob_is_err=False,
                    ).then_inc(scattered[s.q4], 16)

            def body(it):
                if s := it(0):
                    gather(s)
                if it.i == 6 and it.reg is None:
                    pool.wait_ge(zero_filled, 16 * (SLOTS // 2048))
                if s := it(6):
                    scatter(s)

            pipeline(pool, LAST, body)
            for k in range(4):
                pool.wait_ge(scattered[k], 16 * 2 * C * B // 4)

        @block.scalar
        def _(act):
            def gates(s):
                act.wait_ge(gates_ready, s.b + 1)
                if s.after(2):
                    act.wait_ge(scanned, s.b - 1)
                act.activation(hold[:, s.q2, :], gate_ps[:, :L], ACT.Sigmoid, bias=bias[:, 0:1], scale=-1.0)
                act.activation(cand[:, s.q2, :], cand_ps[:, :L], ACT.Tanh, bias=bias[:, 1:2]).then_inc(gates_acted, 1)

            def scores(s):
                act.wait_ge(top_ready, s.b + 1)
                act.activation(keep["top_scores"][:, bass.ds(s.tile(), C), :], top8[:, s.q2, :, 0:2],
                               ACT.Sigmoid).then_inc(scored, 1)

            def copy_x3t(s):
                act.wait_ge(x3t_ready, s.b + 1)
                if s.after(2):
                    act.wait_ge(x_stored[s.q2], s.b2 * 16)
                    act.wait_ge(logits_ready, s.b - 1)
                act.copy(x3_t[:, s.q2, :], x3t_ps[:, :L]).then_inc(x3t_copied, 1)

            def copy_xt(s):
                act.wait_ge(xt_ready, s.b + 1)
                if s.after(2):
                    act.wait_ge(gates_ready, s.b - 1)
                act.copy(xn_t[:, s.q2, :], xt_ps[:, :L]).then_inc(xt_copied, 1)

            def norm(now, which, dest, rows, ready):
                for c in range(C):
                    last = act.activation(dest[:, c, :], rows(c), ACT.Identity, bias=shift[:, 1 - now.q2, which, c:c + 1],
                                          scale=rstd[:, 1 - now.q2, which, c:c + 1])
                last.then_inc(ready, 1)

            def h_rows(s):
                return lambda c: h[:, bass.ds(s.tile() + c, 1), :].rearrange("p a d -> p (a d)")

            def scale_values(s):
                if s.after(2):
                    wait_apart(act, set_up, h_summed, s.b - 1)
                for c in range(C):
                    last = act.activation(vn[:, s.q2, c, :], w_cv[:, c, :], ACT.Copy,
                                          scale=v_scale[:, bass.ds(s.tile() + c, 1)])
                last.then_inc(values_scaled, 1)

            def body(it):
                now = it.now
                if now.after(1):
                    wait_apart(act, set_up, shift_ready, now.b)
                if s := it(4):
                    if s.after(2):
                        wait_apart(act, set_up, xt_ready, s.b - 1)
                    norm(now, 1, xn[:, s.q2, :, :], h_rows(s), x_ready)
                if s := it(5):
                    if s.after(4):
                        wait_apart(act, set_up, scattered[s.q4], s.b4 * 16 * 2 * C)
                    norm(now, 2, x3[:, s.q4, :, :], h_rows(s), x3_ready)
                if s := it(4):
                    copy_xt(s)
                if s := it(5):
                    copy_x3t(s)
                if s := it(4):
                    gates(s)
                if s := it(6):
                    scores(s)
                if s := it(2):
                    act.wait_ge(gathered[s.q4], s.b4 * 64 + 64)
                    if s.after(2):
                        act.wait_ge(h_summed, s.b - 1)
                    norm(now, 0, gn[:, s.q2, :, :], lambda c: g[:, s.q4, c, :], normed)
                if s := it(1):
                    scale_values(s)
                act.wait_ge(stats_ready, now.b + 1)
                act.activation(std[:, now.q2, :, :], moments[:, now.q2, :, :, 1], ACT.Sqrt,
                               bias=eps[:T, :]).then_inc(std_ready, 1)

            pipeline(act, LAST, body)

        @block.tensor
        def _(pe):
            pe.matmul(rank_ps[:T, :C * E], ones[:, :], no_mask[:, :], start=True, stop=False, skip_group_check=True)

            def transpose_scan(s):
                pe.wait_ge(scanned, s.b + 1)
                if s.after(1):
                    pe.wait_ge(scan_added, s.b)
                for c in range(C):
                    last = pe.transpose(scan_ps[:T, c * D:(c + 1) * D], scan[:, s.q2, c * T:(c + 1) * T], ident[:, :])
                last.then_inc(scan_t_ready, 1)

            def add_pairs(which, first, past, masks):
                return pe.matmul(rank_ps[:T, first * E:past * E].rearrange("p (c e) -> p c e", e=E), which[:, :],
                                 masks, start=False, stop=False, skip_group_check=True)

            def of_chunk(s, k, times):
                return bc(mask[:, s.q2, k, :], 1, times, [T, times, E])

            def rank(s):
                pe.wait_ge(masked, s.b + 1)
                for k in range(C - 1):
                    add_pairs(ones, k + 1, C, of_chunk(s, k, C - 1 - k))
                add_pairs(before, 0, C, mask[:, s.q2, :, :]).then_inc(rank_ready, 1)

            def count_rest(s):
                pe.wait_ge(rank_read, s.b + 1)
                for k in range(1, C):
                    add_pairs(ones, 0, k, of_chunk(s, k, k))
                add_pairs(not_before, 0, C, mask[:, s.q2, :, :]).then_inc(rank_next, 1)

            def transpose_x3(s):
                pe.wait_ge(x3_ready, s.b + 1)
                if s.after(1):
                    pe.wait_ge(x3t_copied, s.b)
                for c in range(C):
                    last = pe.transpose(x3t_ps[:, c * T:(c + 1) * T], x3[:, s.q4, c, :], ident[:T, :T])
                last.then_inc(x3t_ready, 1)

            def transpose_x(s):
                pe.wait_ge(x_ready, s.b + 1)
                if s.after(1):
                    pe.wait_ge(xt_copied, s.b)
                for c in range(C):
                    last = pe.transpose(xt_ps[:, c * T:(c + 1) * T], xn[:, s.q2, c, :], ident[:T, :T])
                last.then_inc(xt_ready, 1)

            def logits(s):
                pe.wait_ge(x3t_copied, s.b + 1)
                if s.after(1):
                    pe.wait_ge(masked, s.b)
                for c in range(C):
                    last = pe.matmul(logit_ps[:T, c * D:(c + 1) * D], x3_t[:, s.q2, c * T:(c + 1) * T],
                                     w_t[:, 2, :], start=True, stop=True)
                last.then_inc(logits_ready, 1)

            def gate_products(s):
                pe.wait_ge(xt_copied, s.b + 1)
                if s.after(1):
                    pe.wait_ge(gates_acted, s.b)
                pe.matmul(gate_ps[:, :L], w_t[:, 0, :], xn_t[:, s.q2, :], start=True, stop=True)
                pe.matmul(cand_ps[:, :L], w_t[:, 1, :], xn_t[:, s.q2, :], start=True, stop=True).then_inc(gates_ready, 1)

            def body(it):
                if s := it(4):
                    transpose_x(s)
                if s := it(5):
                    transpose_x3(s)
                if s := it(4):
                    gate_products(s)
                if s := it(6):
                    rank(s)
                if s := it(5):
                    logits(s)
                if s := it(4):
                    transpose_scan(s)
                if s := it(6):
                    count_rest(s)

            pipeline(pe, LAST, body)

        @block.vector
        def _(dve):
            n = Count(dve_done)

            def moments_of(rows, norm, now):
                taken = [n.done(dve.bn_stats(stats[:, norm, c, :], rows(c))) for c in range(C)]
                for c in range(C):
                    wait_apart(dve, set_up, dve_done, taken[c])
                    n.done(dve.bn_aggr(moments[:, now.q2, norm, c, :], stats[:, norm, c, :]))

            def row_moments(s, now):
                dve.wait_ge(gathered[s.q4], s.b4 * 64 + 64)
                moments_of(lambda c: g[:, s.q4, c, :], 0, now)

            def sum_h(s):
                dve.wait_ge(values_scaled, s.b + 1)
                with_beta = n.done(dve.tensor_tensor(vn[:, s.q2, :, :], vn[:, s.q2, :, :],
                                                     bc(beta[:, :], 1, C, [T, C, D]), ALU.add))
                dve.wait_ge(normed, s.b + 1)
                g_done = n.done(dve.tensor_tensor(gn[:, s.q2, :, :], gn[:, s.q2, :, :],
                                                  bc(gamma_g[:, :], 1, C, [T, C, D]), ALU.mult))
                dve.wait_ge(dve_done, with_beta)
                for c in range(C):
                    v_done = n.done(dve.scalar_tensor_tensor(
                        out=vn[:, s.q2, c, :], in0=b_cv[:, c, :], scalar=v_rstd[:, bass.ds(s.tile() + c, 1)],
                        in1=vn[:, s.q2, c, :], op0=ALU.mult, op1=ALU.add))
                dve.wait_ge(dve_done, v_done)
                dve.tensor_tensor(h[:, bass.ds(s.tile(), C), :], gn[:, s.q2, :, :], vn[:, s.q2, :, :],
                                  ALU.add).then_inc(h_summed, 1)

            def h_moments(s, now):
                wait_apart(dve, set_up, h_summed, s.b + 1)
                moments_of(lambda c: h[:, bass.ds(s.tile() + c, 1), :], 1, now)

            def scan_gates(s):
                dve.wait_ge(gates_acted, s.b + 1)
                flown = n.done(dve.scalar_tensor_tensor(out=inflow[:, s.q2, :], in0=hold[:, s.q2, :], scalar=1.0,
                                                        in1=cand[:, s.q2, :], op0=ALU.subtract, op1=ALU.mult))
                dve.wait_ge(dve_done, flown)
                if s.after(2):
                    dve.wait_ge(scan_t_ready, s.b - 1)
                dve.tensor_tensor_scan(out=scan[:, s.q2, :], data0=hold[:, s.q2, :], data1=inflow[:, s.q2, :],
                                       initial=0.0, op0=ALU.mult, op1=ALU.add).then_inc(scanned, 1)

            def add_scan(s, now):
                dve.wait_ge(scan_t_ready, s.b + 1)
                here = h[:, bass.ds(s.tile(), C), :]
                dve.tensor_tensor(here, here, scan_ps[:T, :C * D].rearrange("p (c d) -> p c d", c=C),
                                  ALU.subtract).then_inc(scan_added, 1)
                wait_apart(dve, set_up, scan_added, s.b + 1)
                moments_of(lambda c: h[:, bass.ds(s.tile() + c, 1), :], 2, now)

            def route(s):
                wait_apart(dve, set_up, logits_ready, s.b + 1)
                found = []
                for c in range(C):
                    top = dve.max(out=top8[:, s.q2, c, :], in_=logit_ps[:T, c * D:c * D + E])
                    if c < C - 1:
                        found.append(n.done(top))
                top.then_inc(top_ready, 1)
                for c in range(C):
                    if c < C - 1:
                        wait_apart(dve, set_up, dve_done, found[c])
                    else:
                        wait_apart(dve, set_up, top_ready, s.b + 1)
                    placed = n.done(dve.max_index(out=top_i[:, s.q2, c, :], in_max=top8[:, s.q2, c, :],
                                                  in_values=logit_ps[:T, c * D:c * D + E]))
                dve.wait_ge(dve_done, placed)
                known = n.done(dve.tensor_copy(expert[:, s.q2, :, :], top_i[:, s.q2, :, 0:2]))
                dve.wait_ge(dve_done, known)
                lit = n.done(dve.tensor_tensor(
                    hot[:, s.q2, :, :, :].rearrange("p c k e -> p (c k) e"),
                    bc(expert_no[:, :], 1, 2 * C, [T, 2 * C, E]),
                    bc(expert[:, s.q2, :, :].rearrange("p c k -> p (c k)"), 2, E, [T, 2 * C, E]), ALU.is_equal))
                dve.wait_ge(dve_done, lit)
                dve.tensor_tensor(mask[:, s.q2, :, :], hot[:, s.q2, :, 0, :], hot[:, s.q2, :, 1, :],
                                  ALU.add).then_inc(masked, 1)

            def read_rank(s):
                dve.wait_ge(rank_ready, s.b + 1)
                dve.tensor_tensor(rank_e[:, :, :, :], hot[:, s.q2, :, :, :],
                                  bc(rank_ps[:T, :C * E].rearrange("p (c e) -> p c e", c=C), 2, 2, [T, C, 2, E]),
                                  ALU.mult).then_inc(rank_read, 1)
                dve.wait_ge(rank_read, s.b + 1)
                dve.tensor_reduce(pos[:, :, :], rank_e[:, :, :, :], axis=AX.X, op=ALU.add).then_inc(pos_ready, 1)

            def place(s):
                dve.wait_ge(pos_ready, s.b + 1)
                n.done(dve.tensor_scalar(late[:, :, :], pos[:, :, :], float(CAP), FAR, ALU.is_ge, ALU.mult))
                both = n.done(dve.scalar_tensor_tensor(out=slot_0[:, :, :], in0=expert[:, s.q2, :, :], scalar=float(CAP),
                                                       in1=pos[:, :, :], op0=ALU.mult, op1=ALU.add))
                dve.wait_ge(dve_done, both)
                slots = keep["slots"][:, bass.ds(s.tile(), C), :]
                put = n.done(dve.tensor_tensor(slots, slot_0[:, :, :], late[:, :, :], ALU.add))
                wait_apart(dve, set_up, dve_done, put)
                dve.tensor_copy(slot_i[:, s.q4, :].rearrange("p (c k) -> p c k", c=C), slots).then_inc(slot_ready, 1)

            def body(it):
                now = it.now
                if s := it(3):
                    sum_h(s)
                    h_moments(s, now)
                if s := it(1):
                    row_moments(s, now)
                if s := it(6):
                    route(s)
                if s := it(4):
                    scan_gates(s)
                if s := it(6):
                    read_rank(s)
                    place(s)
                if s := it(4):
                    add_scan(s, now)
                dve.wait_ge(dve_done, n.now())
                dve.memset(flag[:, :], 0.0).then_inc(stats_ready, 1)
                dve.wait_ge(std_ready, now.b + 1)
                got = n.done(dve.reciprocal(rstd[:, now.q2, :, :], std[:, now.q2, :, :]))
                dve.wait_ge(dve_done, got)
                dve.scalar_tensor_tensor(out=shift[:, now.q2, :, :], in0=moments[:, now.q2, :, :, 0], scalar=-1.0,
                                         in1=rstd[:, now.q2, :, :], op0=ALU.mult, op1=ALU.mult).then_inc(shift_ready, 1)

            pipeline(dve, LAST, body, count=n)


def setup(nc, io, keep, own):
    with ExitStack() as ctx:
        def sb(name, shape, dt=F32):
            return ctx.enter_context(nc.sbuf_tensor(name, shape, dt))

        def sem(name):
            return ctx.enter_context(nc.semaphore(name))

        ident, w_t = keep["ident"], keep["w_t"]
        w_cv, b_cv, beta, gamma_g = own["w_cv"], own["b_cv"], own["beta"], own["gamma_g"]
        v_scale, v_rstd, ids_t, bias, banks = (own[k] for k in ("v_scale", "v_rstd", "ids_t", "bias", "banks"))
        raw = sb("raw", [128, 6, 128])
        ids_i = sb("ids_i", [NT, T], I32)
        ids_f = sb("ids_f", [NT, T])
        value = sb("value", [NT, T])
        value_t = sb("value_t", [T, NT])
        wv = sb("wv", [T, C, D])
        bv = sb("bv", [T, C, D])
        gamma_v = sb("gamma_v", [T, D])
        betas = sb("betas", [T, 2, D])
        cross = sb("cross", [T, C, D])
        st = sb("st", [T, 2, C, 6])
        mv = sb("mv", [T, 2, C, 2])
        cov = sb("cov", [T, C])
        var = sb("var", [T, NT])
        term = sb("term", [T, NT])
        square = sb("square", [T, NT])
        loaded, values_loaded, made, transposed, copied, done, rooted, var_ready = (sem(n) for n in (
            "loaded", "values_loaded", "made", "transposed", "copied", "done", "rooted", "var_ready"))
        weights = [(io["L0_attn_Wg"], 128), (io["L0_attn_Wc"], 128), (io["L0_ffn_gate_w"], E), (io["L1_attn_q_w"], 128),
                   (io["L1_attn_kv_w"][0:128, :], 128), (io["L1_attn_kv_w"][128:256, :], 128)]
        block = ctx.enter_context(nc.Block())

        @block.sync
        def _(sp):
            sp.dma_start(ids_i[:, :], io["x"].rearrange("b (c p) -> (b c) p", c=C)).then_inc(values_loaded, 16)
            sp.dma_start(value[:, :], io["fside_BS_value"].rearrange("b (c p) -> (b c) p", c=C)).then_inc(values_loaded, 16)
            sp.dma_start(wv[:, :, :], io["L0_tok_w_val"].rearrange("(c p) d -> p c d", c=C)).then_inc(values_loaded, 16)
            sp.dma_start(bv[:, :, :], io["L0_tok_b_val"].rearrange("(c p) d -> p c d", c=C)).then_inc(values_loaded, 16)
            for dest, name in ((gamma_v[:, :], "L0_tok_gamma_v"), (gamma_g[:, :], "L0_tok_gamma_g"),
                               (betas[:, 0, :], "L0_tok_beta_g"), (betas[:, 1, :], "L0_tok_beta_v")):
                sp.dma_start(dest, io[name].partition_broadcast(T)).then_inc(values_loaded, 16)
            for k, (w, rows) in enumerate(weights):
                sp.dma_start(raw[:rows, k, :], w).then_inc(loaded, 16)
            sp.dma_start(bias[:, 0:1], io["L0_attn_bg"].rearrange("(p a) -> p a", a=1)).then_inc(loaded, 16)
            sp.dma_start(bias[:, 1:2], io["L0_attn_bc"].rearrange("(p a) -> p a", a=1)).then_inc(loaded, 16)

        @block.gpsimd
        def _(pool):
            pool.memset(own["zeros"][:, :], 0.0).then_inc(made, 1)
            pool.memset(own["flag"][:, :], 0.0).then_inc(own["set_up"], 1)
            pool.memset(ident[:, :], 0.0).then_inc(made, 1)
            pool.memset(own["ones"][:, :], 1.0).then_inc(made, 1)
            pool.memset(own["before"][:, :], 1.0).then_inc(made, 1)
            pool.memset(own["not_before"][:, :], 1.0).then_inc(made, 1)
            pool.wait_ge(made, 5)
            pool.affine_select(out=ident[:, :], in_=ident[:, :], compare_op=ALU.not_equal, fill=1.0,
                               base=0, pattern=[[-1, 128]], channel_multiplier=1).then_inc(made, 1)
            pool.affine_select(out=own["before"][:, :], in_=own["before"][:, :], compare_op=ALU.is_gt, fill=0.0,
                               base=0, pattern=[[1, T]], channel_multiplier=-1).then_inc(made, 1)
            pool.affine_select(out=own["not_before"][:, :], in_=own["not_before"][:, :], compare_op=ALU.is_ge, fill=0.0,
                               base=0, pattern=[[-1, T]], channel_multiplier=1).then_inc(made, 1)
            pool.iota(own["expert_no"][:, :], pattern=[[1, E]], base=0, channel_multiplier=0,
                      allow_small_or_imprecise_dtypes=True).then_inc(made, 1)
            pool.memset(w_t[:, 2, E:], 0.0).then_inc(made, 1)
            pool.memset(own["eps"][:, :], EPS).then_inc(made, 1)
            pool.memset(own["moments"][:, :, :, :, :], 1.0).then_inc(made, 1)
            pool.memset(own["no_mask"][:, :], 0.0).then_inc(made, 1)
            pool.wait_ge(made, 13)

        @block.tensor
        def _(pe):
            pe.wait_ge(made, 6)
            pe.wait_ge(loaded, 16 * 8)
            for k, (_, rows) in enumerate(weights):
                pe.transpose(banks[k][:, :rows], raw[:rows, k, :], ident[:rows, :rows]).then_inc(transposed, 1)
            pe.wait_ge(copied, 1)
            pe.transpose(banks[6][:T, :NT], ids_f[:, :], ident[:, :]).then_inc(transposed, 1)
            pe.transpose(banks[7][:T, :NT], value[:, :], ident[:, :]).then_inc(transposed, 1)

        @block.scalar
        def _(act):
            act.wait_ge(var_ready, 1)
            act.wait_ge(made, 13)
            act.activation(var[:, :], var[:, :], ACT.Sqrt, bias=own["eps"][:T, :]).then_inc(rooted, 1)

        @block.vector
        def _(dve):
            n = Count(done)

            def link(ins):
                dve.wait_ge(done, n.done(ins))

            dve.wait_ge(values_loaded, 16 * 8)
            dve.tensor_copy(ids_f[:, :], ids_i[:, :]).then_inc(copied, 1)
            for c in range(C):
                n.done(dve.bn_stats(st[:, 0, c, :], wv[:, c, :]))
                link(dve.bn_stats(st[:, 1, c, :], bv[:, c, :]))
            for c in range(C):
                n.done(dve.bn_aggr(mv[:, 0, c, :], st[:, 0, c, :]))
                link(dve.bn_aggr(mv[:, 1, c, :], st[:, 1, c, :]))
            n.done(dve.tensor_tensor(wv[:, :, :], wv[:, :, :], mv[:, 0, :, 0:1].to_broadcast([T, C, D]), ALU.subtract))
            link(dve.tensor_tensor(bv[:, :, :], bv[:, :, :], mv[:, 1, :, 0:1].to_broadcast([T, C, D]), ALU.subtract))
            link(dve.tensor_tensor(cross[:, :, :], wv[:, :, :], bv[:, :, :], ALU.mult))
            link(dve.tensor_reduce(cov[:, :], cross[:, :, :], axis=AX.X, op=ALU.add))
            gv = bc(gamma_v[:, :], 1, C, [T, C, D])
            n.done(dve.tensor_tensor(w_cv[:, :, :], wv[:, :, :], gv, ALU.mult))
            n.done(dve.tensor_tensor(b_cv[:, :, :], bv[:, :, :], gv, ALU.mult))
            n.done(dve.tensor_tensor(beta[:, :], betas[:, 0, :], betas[:, 1, :], ALU.add))
            dve.wait_ge(transposed, 8)
            n.done(dve.tensor_copy(ids_t[:, :], banks[6][:T, :NT]))
            link(dve.tensor_copy(value_t[:, :], banks[7][:T, :NT]))

            def by_chunk(x):
                return x.rearrange("p (b c) -> p b c", c=C)

            def over_batches(x):
                return bc(x, 1, B, [T, B, C])

            link(dve.tensor_tensor(square[:, :], value_t[:, :], value_t[:, :], ALU.mult))
            n.done(dve.tensor_tensor(by_chunk(square[:, :]), by_chunk(square[:, :]), over_batches(mv[:, 0, :, 1]), ALU.mult))
            link(dve.tensor_tensor(by_chunk(term[:, :]), by_chunk(value_t[:, :]), over_batches(cov[:, :]), ALU.mult))
            link(dve.scalar_tensor_tensor(out=var[:, :], in0=term[:, :], scalar=2.0 / D, in1=square[:, :],
                                          op0=ALU.mult, op1=ALU.add))
            link(dve.tensor_tensor(by_chunk(var[:, :]), by_chunk(var[:, :]), over_batches(mv[:, 1, :, 1]), ALU.add))
            dve.tensor_scalar(var[:, :], var[:, :], 0.0, None, ALU.max).then_inc(var_ready, 1)
            for k, (_, rows) in enumerate(weights):
                n.done(dve.tensor_copy(w_t[:, k, :rows], banks[k][:, :rows]))
            dve.wait_ge(loaded, 16 * 8)
            n.done(dve.tensor_scalar(bias[:, 0:1], bias[:, 0:1], -1.0, None, ALU.mult))
            dve.wait_ge(rooted, 1)
            link(dve.reciprocal(v_rstd[:, :], var[:, :]))
            link(dve.tensor_tensor(v_scale[:, :], value_t[:, :], v_rstd[:, :], ALU.mult))


def experts(nc, io, keep, dram):
    with ExitStack() as ctx:
        def sb(name, shape, dt=F32):
            return ctx.enter_context(nc.sbuf_tensor(name, shape, dt))

        def sem(name):
            return ctx.enter_context(nc.semaphore(name))

        h = keep["h"]
        shared = sb("shared", [D, 3, D])
        xt = sb("xt", [D, 4, L])
        xs = sb("xs", [128, 4, 4, D])
        xst = sb("xst", [D, 2, 4 * 128])
        w1 = sb("w1", [D, 4, 2, HID])
        w3 = sb("w3", [D, 4, 2, HID])
        w2 = sb("w2", [2 * HID, 4, D])
        s_sig = sb("s_sig", [D, 2, L])
        s_hid = sb("s_hid", [D, 2, L])
        e_sig = sb("e_sig", [2 * HID, 2, CAP])
        e_hid = sb("e_hid", [2 * HID, 2, CAP])
        y = sb("y", [128, 2, 4, D])
        banks = [ctx.enter_context(nc.psum_tensor(f"b_bank{k}", [128, 512], F32)) for k in range(5)]
        xst_ps, s1_ps, s3_ps, hid_ps, sum_ps = banks
        y_ps = ctx.enter_context(nc.psum_tensor("y_ps", [128, 2, 512], F32))
        loaded = [sem(f"e_loaded{k}") for k in range(4)]
        y_stored = [sem(f"y_stored{k}") for k in range(2)]
        (shared_loaded, slots_turned, turned_copied, shared_up, s_sig_ready, s_silu, s_hid_ready, hidden_up, e_sig_ready,
         e_silu, e_hid_ready, shared_down, shared_added, y_ready, y_copied) = (sem(k) for k in (
            "shared_loaded slots_turned turned_copied shared_up s_sig_ready s_silu s_hid_ready hidden_up e_sig_ready "
            "e_silu e_hid_ready shared_down shared_added y_ready y_copied").split())
        block = ctx.enter_context(nc.Block())
        LAST = B + 4

        @block.sync
        def _(sp):
            for k, name in enumerate(("L0_ffn_sw1", "L0_ffn_sw3", "L0_ffn_sw2")):
                sp.dma_start(shared[:, k, :], io[name]).then_inc(shared_loaded, 16)
            x_slots = dram["x_slots"].rearrange("(j u p) d -> j p u d", u=4, p=128)
            y_slots = dram["y_slots"].rearrange("(j u p) d -> j p u d", u=4, p=128)
            w1_pairs = io["L0_ffn_w1"].rearrange("(j e) d h -> j d e h", e=2)
            w3_pairs = io["L0_ffn_w3"].rearrange("(j e) d h -> j d e h", e=2)
            w2_pairs = io["L0_ffn_w2"].rearrange("(j e) h d -> j (e h) d", e=2)

            def pair(x, s, pattern="j p u d -> p (j u) d"):
                return x[bass.ds(s.b, 1)].rearrange(pattern)

            def load(s):
                if s.after(4):
                    sp.wait_ge(y_ready, s.b - 3)
                    sp.wait_ge(shared_up, s.b - 3)
                into = loaded[s.q4]
                sp.dma_start(xs[:, s.q4, :, :], pair(x_slots, s)).then_inc(into, 16)
                sp.dma_start(xt[:, s.q4, :], pair(dram["x_t"], s, "j d l -> d (j l)")).then_inc(into, 16)
                sp.dma_start(w1[:, s.q4, :, :], pair(w1_pairs, s)).then_inc(into, 16)
                sp.dma_start(w3[:, s.q4, :, :], pair(w3_pairs, s)).then_inc(into, 16)
                sp.dma_start(w2[:, s.q4, :], pair(w2_pairs, s, "j r d -> r (j d)")).then_inc(into, 16)

            def store(s):
                sp.wait_ge(y_copied, s.b + 1)
                sp.dma_start(pair(y_slots, s), y[:, s.q2, :, :]).then_inc(y_stored[s.q2], 16)

            def body(it):
                if s := it(0):
                    load(s)
                if s := it(5):
                    store(s)

            pipeline(sp, LAST, body)
            for k in range(2):
                sp.wait_ge(y_stored[k], 16 * B // 2)

        @block.tensor
        def _(pe):
            pe.wait_ge(shared_loaded, 48)

            def turn_slots(s):
                pe.wait_ge(loaded[s.q4], s.b4 * 80 + 80)
                if s.after(1):
                    pe.wait_ge(turned_copied, s.b)
                for u in range(4):
                    last = pe.transpose(xst_ps[:, u * 128:(u + 1) * 128], xs[:, s.q4, u, :], keep["ident"][:, :])
                last.then_inc(slots_turned, 1)

            def up_shared(s):
                if s.after(1):
                    pe.wait_ge(s_hid_ready, s.b)
                pe.matmul(s1_ps[:, :L], shared[:, 0, :], xt[:, s.q4, :], start=True, stop=True)
                pe.matmul(s3_ps[:, :L], shared[:, 1, :], xt[:, s.q4, :], start=True, stop=True).then_inc(shared_up, 1)

            def up_experts(s):
                pe.wait_ge(turned_copied, s.b + 1)
                if s.after(1):
                    pe.wait_ge(e_hid_ready, s.b)
                for half, w in ((0, w1), (1, w3)):
                    for e in range(2):
                        last = pe.matmul(hid_ps[e * HID:(e + 1) * HID, half * CAP:(half + 1) * CAP], w[:, s.q4, e, :],
                                         xst[:, s.q2, e * CAP:(e + 1) * CAP], start=True, stop=True)
                last.then_inc(hidden_up, 1)

            def down_shared(s):
                pe.wait_ge(s_hid_ready, s.b + 1)
                if s.after(1):
                    pe.wait_ge(shared_added, s.b)
                for c in range(C):
                    last = pe.matmul(sum_ps[:T, c * D:(c + 1) * D], s_hid[:, s.q2, c * T:(c + 1) * T], shared[:, 2, :],
                                     start=True, stop=True)
                last.then_inc(shared_down, 1)

            def down_experts(s):
                pe.wait_ge(e_hid_ready, s.b + 1)
                if s.after(1):
                    pe.wait_ge(y_copied, s.b)
                for u in range(4):
                    rows = slice(u // 2 * HID, (u // 2 + 1) * HID)
                    last = pe.matmul(y_ps[:, u // 2, u % 2 * D:(u % 2 + 1) * D], e_hid[rows, s.q2, u % 2 * 128:(u % 2 + 1) * 128],
                                     w2[rows, s.q4, :], start=True, stop=True)
                last.then_inc(y_ready, 1)

            def body(it):
                if s := it(3):
                    turn_slots(s)
                    up_shared(s)
                if s := it(4):
                    down_shared(s)
                if s := it(3):
                    up_experts(s)
                if s := it(4):
                    down_experts(s)

            pipeline(pe, LAST, body)

        @block.scalar
        def _(act):
            def body(it):
                if s := it(3):
                    act.wait_ge(slots_turned, s.b + 1)
                    if s.after(2):
                        act.wait_ge(hidden_up, s.b - 1)
                    act.copy(xst[:, s.q2, :], xst_ps[:, :]).then_inc(turned_copied, 1)
                    act.wait_ge(shared_up, s.b + 1)
                    if s.after(2):
                        act.wait_ge(s_silu, s.b - 1)
                    act.activation(s_sig[:, s.q2, :], s1_ps[:, :L], ACT.Sigmoid).then_inc(s_sig_ready, 1)
                    act.wait_ge(hidden_up, s.b + 1)
                    if s.after(2):
                        act.wait_ge(e_silu, s.b - 1)
                    act.activation(e_sig[:, s.q2, :], hid_ps[:, :CAP], ACT.Sigmoid).then_inc(e_sig_ready, 1)
                if s := it(4):
                    act.wait_ge(y_ready, s.b + 1)
                    if s.after(2):
                        act.wait_ge(y_stored[s.q2], s.b2 * 16)
                    act.copy(y[:, s.q2, :, :].rearrange("p (e u) d -> p e (u d)", e=2),
                             y_ps[:, :, :2 * D]).then_inc(y_copied, 1)

            pipeline(act, LAST, body)

        @block.vector
        def _(dve):
            def body(it):
                if s := it(3):
                    dve.wait_ge(s_sig_ready, s.b + 1)
                    if s.after(2):
                        dve.wait_ge(shared_down, s.b - 1)
                    dve.tensor_tensor(s_hid[:, s.q2, :], s_sig[:, s.q2, :], s1_ps[:, :L], ALU.mult).then_inc(s_silu, 1)
                    dve.wait_ge(s_silu, s.b + 1)
                    dve.tensor_tensor(s_hid[:, s.q2, :], s_hid[:, s.q2, :], s3_ps[:, :L], ALU.mult).then_inc(s_hid_ready, 1)
                    dve.wait_ge(e_sig_ready, s.b + 1)
                    if s.after(2):
                        dve.wait_ge(y_ready, s.b - 1)
                    dve.tensor_tensor(e_hid[:, s.q2, :], e_sig[:, s.q2, :], hid_ps[:, :CAP], ALU.mult).then_inc(e_silu, 1)
                    dve.wait_ge(e_silu, s.b + 1)
                    dve.tensor_tensor(e_hid[:, s.q2, :], e_hid[:, s.q2, :], hid_ps[:, CAP:], ALU.mult).then_inc(e_hid_ready, 1)
                if s := it(4):
                    dve.wait_ge(shared_down, s.b + 1)
                    here = h[:, bass.ds(s.tile(), C), :]
                    dve.tensor_tensor(here, here, sum_ps[:T, :].rearrange("p (c d) -> p c d", c=C),
                                      ALU.add).then_inc(shared_added, 1)

            pipeline(dve, LAST, body)


PIECES = ((0, 1, 2, 0, 1, 0), (0, 0, 0, 1, 1, 2))
NROW = 6 * DH
SROW = NROW + 3


def attention(nc, io, keep, dram, out):
    with ExitStack() as ctx:
        def sb(name, shape, dt=F32):
            return ctx.enter_context(nc.sbuf_tensor(name, shape, dt))

        def pb(name, shape, dt=F32):
            return ctx.enter_context(nc.psum_tensor(name, shape, dt))

        def sem(name):
            return ctx.enter_context(nc.semaphore(name))

        h, ident, w_t, slots = keep["h"], keep["ident"], keep["w_t"], keep["slots"]
        share = sb("share", [T, NT, 2])
        slots_i = sb("slots_i", [T, NT, 2], I32)
        total = sb("total", [T, NT])
        qk_w = sb("qk_w", [D, 2, D])
        v_new = sb("v_new", [T, C, H, DH + 1])
        identb = sb("identb", [T, T], BF16)
        minus_half = sb("minus_half", [T, C])
        q_st = sb("q_st", [SROW, 4, H, L], BF16)
        k_st = sb("k_st", [SROW, 4, H, L], BF16)
        v = sb("v", [T, 4, C, H, DH + 1])
        y_idx = sb("y_idx", [T, 2, C * 2], I32)
        y = sb("y_pairs", [T, 2, C * 2, D])
        c_stats = sb("c_stats", [T, 2, C, 6])
        c_mom = sb("c_mom", [T, 2, 2, C, 2])
        c_var = sb("c_var", [T, 2, C])
        c_rstd = sb("c_rstd", [T, 2, C])
        c_gain = sb("c_gain", [T, C])
        c_shift = sb("c_shift", [T, 2, C])
        x4 = sb("x4", [T, C, D])
        x4_t = sb("x4_t", [D, L])
        parts = [sb(f"{a}_parts", [D, 3, L], BF16) for a in "qk"]
        rest = sb("rest", [D, L])
        top = sb("top", [T, 2, 4, C])
        top_rest = sb("top_rest", [T, 4, C])
        top_parts = sb("top_parts", [T, 2, C, 3, 4], BF16)
        top_rows = sb("top_rows", [12, L], BF16)
        p = sb("p", [T, 2, 4, 2, L])
        o_t = sb("o_t", [128, L])
        o_inv = sb("o_inv", [T, C, 4])
        o = sb("o", [T, 2, C, D])
        res = sb("res", [T, C, D])

        max_ps = [pb(f"max_ps{k}", [128, 512]) for k in range(2)]
        s_ps = pb("s_ps", [128, 2, 2, 512])
        o_ps = pb("o_ps", [128, 512])
        misc = pb("misc", [128, 512])

        parts_d = [nc.dram_tensor(f"{a}_parts_d", (2, 3, D, L), BF16, kind="Internal").ap() for a in "qk"]
        v_d = nc.dram_tensor("v_d", (2, T, C * H * (DH + 1)), F32, kind="Internal").ap()
        top_d = nc.dram_tensor("top_d", (2, 12, L), BF16, kind="Internal").ap()

        y_there = [sem(f"y_there{k}") for k in range(2)]
        stacked = [sem(f"stacked{k}") for k in range(4)]
        parts_there = [sem(f"parts_there{k}") for k in range(2)]
        res_there = sem("res_there")
        top_stored = sem("top_stored")
        top_there = [sem(f"top_there{k}") for k in range(2)]
        (c_set, idx_ready, var4_ready, rstd4_ready, shift4_ready, x4_ready, x4t_ready, x4t_copied, v_ready, v_copied,
         q_ready, q1_copied, q_rest, k_ready, k1_copied, k_rest, split, scored, reduced, top_split, top_turned,
         top_copied, products, exps, weighed, o_copied, o_turned, o_normed, h_done, var5_ready, rstd5_ready, gain_ready,
         res_ready, vec_done, pool_done, combined) = (sem("c_" + k) for k in (
            "c_set idx_ready var4_ready rstd4_ready shift4_ready x4_ready x4t_ready x4t_copied v_ready v_copied "
            "q_ready q1_copied q_rest k_ready k1_copied k_rest split scored reduced top_split top_turned "
            "top_copied products exps weighed o_copied o_turned o_normed h_done var5_ready rstd5_ready gain_ready "
            "res_ready vec_done pool_done combined").split())

        def tile(s):
            return s.b2 * C + s.q2 * (NT // 2)

        def done(s, per=1, of=0):
            return s.b * per + (of or per)

        vec_from, pool_from = Count(vec_done), 3
        with nc.Block() as block:
            @block.gpsimd
            def _(pool):
                pool.memset(minus_half[:, :], -0.5).then_inc(pool_done, 1)
                pool.memset(y[:, :, :, :], 0.0).then_inc(pool_done, 1)
                pool.memset(v_new[:, :, :, :], 1.0).then_inc(pool_done, 1)
                pool.wait_ge(pool_done, 3)

            @block.scalar
            def _(act):
                act.copy(identb[:, :], ident[:T, :T]).then_inc(c_set, 1)

            @block.vector
            def _(dve):
                n = vec_from

                def link(ins):
                    dve.wait_ge(vec_done, n.done(ins))

                score = keep["top_scores"]
                n.done(dve.memset(k_st[NROW:SROW, :, :, :], 1.0))
                n.done(dve.memset(o_ps[:, :], 0.0))
                for a in range(2):
                    n.done(dve.tensor_copy(qk_w[:, a, :].rearrange("p (d h) -> p d h", h=H),
                                           w_t[:, 3 + a, :].rearrange("p (h d) -> p d h", h=H)))
                n.done(dve.tensor_copy(slots_i[:, :, :], slots[:, :, :]))
                link(dve.tensor_tensor(total[:, :], score[:, :, 0], score[:, :, 1], ALU.add))
                link(dve.tensor_scalar(total[:, :], total[:, :], 1e-20, None, ALU.add))
                link(dve.reciprocal(total[:, :], total[:, :]))
                link(dve.tensor_tensor(share[:, :, :], score[:, :, :], bc(total[:, :], 2, 2, [T, NT, 2]), ALU.mult))
                link(dve.tensor_scalar(slots[:, :, :], slots[:, :, :], float(SLOTS), 2.5, ALU.is_lt, ALU.mult))
                link(dve.tensor_tensor(share[:, :, :], share[:, :, :], slots[:, :, :], ALU.mult))

        block = ctx.enter_context(nc.Block())
        LAST = B + 5
        UNITS, GROUPS = 4, 2

        @block.gpsimd
        def _(pool):
            n = Count(pool_done)
            n.n = pool_from

            def gather(s, half):
                if half == 0:
                    if s.after(2):
                        pool.wait_ge(combined, s.b - 1)
                        pool.wait_ge(y_there[s.q2], s.b2 * 128)
                    pool.tensor_copy(y_idx[:, s.q2, :].rearrange("p (c k) -> p c k", k=2),
                                     slots_i[:, bass.ds(tile(s), C), :]).then_inc(idx_ready, 1)
                    wait_apart(pool, c_set, idx_ready, done(s))
                for j in range(half * C, half * C + C):
                    pool.indirect_dma_start(
                        out=y[:, s.q2, j, :], out_offset=None, in_=dram["y_slots"],
                        in_offset=bass.IndirectOffsetOnAxis(ap=y_idx[:, s.q2, j:j + 1], axis=0),
                        bounds_check=SLOTS - 1, oob_is_err=False,
                    ).then_inc(y_there[s.q2], 16)

            def root(s, ready, norm, into):
                pool.wait_ge(ready, done(s))
                pool.tensor_tensor(c_rstd[:, norm, :], c_var[:, norm, :], minus_half[:, :], ALU.pow).then_inc(into, 1)

            def split_rest(s, a, ready):
                wait_apart(pool, c_set, ready, done(s))
                second = n.done(pool.tensor_copy(parts[a][:, 1, :], rest[:, :]))
                pool.wait_ge(pool_done, second)
                pool.tensor_tensor(parts[a][:, 2, :], rest[:, :], parts[a][:, 1, :], ALU.subtract).then_inc(split, 1)

            def body(it):
                if s := it(1):
                    root(s, var4_ready, 0, rstd4_ready)
                if s := it(0):
                    gather(s, 0)
                if s := it(6):
                    root(s, var5_ready, 1, rstd5_ready)
                if s := it(0):
                    gather(s, 1)
                if s := it(1):
                    split_rest(s, 0, q_rest)
                    split_rest(s, 1, k_rest)

            pipeline(pool, LAST, body, count=n)

        @block.sync
        def _(sp):
            def move_top(s, g):
                sp.wait_ge(top_copied, done(s, GROUPS, g + 1))
                sp.dma_start(top_d[g, :, :], top_rows[:, :]).then_inc(top_stored, 16)
                sp.wait_ge(top_stored, s.b * 32 + 16 * (g + 1))
                sp.dma_start(q_st[NROW:SROW, s.q4, 4 * g:4 * g + 4, :].rearrange("j h n -> j (h n)"),
                             top_d[g, :, :].rearrange("(j h) n -> j (h n)", j=3)).then_inc(top_there[g], 16)

            def store_parts(s):
                sp.wait_ge(split, done(s, 2))
                sp.dma_start(v_d[s.q2], v_new[:, :, :, :].rearrange("p c h e -> p (c h e)")).then_inc(parts_there[s.q2], 16)
                for a in range(2):
                    sp.dma_start(parts_d[a][s.q2].rearrange("j r n -> r j n"), parts[a][:, :, :]).then_inc(parts_there[s.q2], 16)

            def load_stacks(s):
                wait_apart(sp, c_set, parts_there[s.q2], s.b2 * 48 + 48)
                if s.after(4):
                    wait_apart(sp, c_set, products, (s.b - 2 - s.q2) * 16)
                    wait_apart(sp, c_set, weighed, (s.b - 2 - s.q2) * 4)
                sp.dma_start(v[:, s.q4, :, :, :].rearrange("p c h e -> p (c h e)"), v_d[s.q2]).then_inc(stacked[s.q4], 16)
                for a, st in ((0, q_st), (1, k_st)):
                    row = 0
                    while row < 6:
                        part, many = PIECES[a][row], 1
                        while a == 0 and row + many < 6 and PIECES[a][row + many] == part + many:
                            many += 1
                        sp.dma_start(st[row * DH:(row + many) * DH, s.q4, :, :].rearrange("r h n -> r (h n)"),
                                     parts_d[a][s.q2, part:part + many].rearrange("j (d h) n -> (j d) (h n)", h=H)
                                     ).then_inc(stacked[s.q4], 16)
                        row += many

            def store_res(s):
                sp.wait_ge(res_ready, done(s))
                sp.dma_start(out[bass.ds(s.b2 + s.q2 * (B // 2), 1), :, :].rearrange("b (c p) d -> p (b c) d", p=T),
                             res[:, :, :]).then_inc(res_there, 16)

            def body(it):
                if s := it(5):
                    move_top(s, 1)
                if s := it(2):
                    store_parts(s)
                if s := it(4):
                    move_top(s, 0)
                if s := it(6):
                    store_res(s)
                if s := it(2):
                    load_stacks(s)

            pipeline(sp, LAST, body)
            sp.wait_ge(res_there, 16 * B)

        @block.tensor
        def _(pe):
            class Misc:
                last = None

            def take_misc(it, lag, reader, per=1, of=0):
                if Misc.last:
                    at, was_lag, was_reader, was_per, was_of = Misc.last
                    back = 0 if at is it else 1
                    s = Step(it.i - back - was_lag, it.reg)
                    pe.wait_ge(was_reader, done(s, was_per, was_of))
                Misc.last = (it, lag, reader, per, of)

            def turn_top(it, s, g, lag):
                pe.wait_ge(top_split, done(s, GROUPS, g + 1))
                take_misc(it, lag, top_copied, GROUPS, g + 1)
                for c in range(C):
                    last = pe.matmul(misc[:12, c * T:(c + 1) * T], top_parts[:, g, c, :, :].rearrange("p j h -> p (j h)"),
                                     identb[:, :], start=True, stop=True)
                last.then_inc(top_turned, 1)

            def turn_o(it, s, g, lag):
                pe.wait_ge(o_copied, done(s, GROUPS, g + 1))
                take_misc(it, lag, o_normed, GROUPS, g + 1)
                for c in range(C):
                    last = pe.transpose(misc[:T, c * 128:(c + 1) * 128], o_t[:, c * T:(c + 1) * T], ident[:, :])
                last.then_inc(o_turned, 1)

            def turn_x4(it, s, lag):
                pe.wait_ge(x4_ready, done(s))
                take_misc(it, lag, x4t_copied)
                for c in range(C):
                    last = pe.transpose(misc[:, c * T:(c + 1) * T], x4[:, c, :], ident[:T, :T])
                last.then_inc(x4t_ready, 1)

            def project_v(it, s, lag):
                pe.wait_ge(x4t_copied, done(s))
                take_misc(it, lag, v_copied)
                for c in range(C):
                    last = pe.matmul(misc[:T, c * D:(c + 1) * D], x4_t[:, c * T:(c + 1) * T], w_t[:, 5, :],
                                     start=True, stop=True)
                last.then_inc(v_ready, 1)

            def project(it, s, a, lag):
                take_misc(it, lag, (q_rest, k_rest)[a])
                pe.matmul(misc[:, :L], qk_w[:, a, :], x4_t[:, :],
                          start=True, stop=True).then_inc((q_ready, k_ready)[a], 1)

            def score(s, head, c):
                at = head * C + c
                if head == 0 and c == 0:
                    pe.wait_ge(stacked[s.q4], s.b4 * 160 + 160)
                    pe.wait_ge(stacked[s.q4 ^ 1], s.b4 * 160 + 160)
                if at >= 2 or s.after(1):
                    pe.wait_ge(reduced, s.b * 32 + at - 1)
                pe.matmul(max_ps[at % 2][:T, :L], q_st[:NROW, s.q4, head, c * T:(c + 1) * T], k_st[:NROW, s.q4 ^ 1, head, :],
                          start=True, stop=True).then_inc(scored, 1)

            def product(s, t):
                unit, head = t // 4, t // 8 * 4 + t % 4
                if t % 8 == 0:
                    pe.wait_ge(top_there[t // 8], done(s) * 16)
                if t >= 2 or s.after(1):
                    pe.wait_ge(exps, s.b * 16 + t - 1)
                for k in range(2):
                    c = unit % 2 * 2 + k
                    last = pe.matmul(s_ps[:T, t % 2, k, :L], k_st[:, s.q4 ^ 1, head, c * T:(c + 1) * T], q_st[:, s.q4, head, :],
                                     start=True, stop=True)
                last.then_inc(products, 1)

            def weigh(s, unit, k):
                if k == 0:
                    pe.wait_ge(exps, s.b * 16 + 4 * unit + 4)
                    if unit % 2 == 0:
                        if unit == 0:
                            if s.after(1):
                                pe.wait_ge(o_copied, s.b * 2)
                        else:
                            pe.wait_ge(o_copied, s.b * 2 + 1)
                c = unit % 2 * 2 + k
                for j in range(4):
                    head = unit // 2 * 4 + j
                    last = pe.matmul(o_ps[32 * j:32 * j + DH + 1, :L], v[:, s.q4 ^ 1, c, head, :], p[:, unit % 2, j, k, :],
                                     start=c == 0, stop=c == 3, skip_group_check=True)
                if k == 1:
                    last.then_inc(weighed, 1)

            def body(it):
                maxima, before, now = it(4), it(6), it(5)
                for t in range(16):
                    if now:
                        product(now, t)
                    if maxima:
                        score(maxima, t // 2, t % 2 * 2)
                        score(maxima, t // 2, t % 2 * 2 + 1)
                    if t % 4 >= 2:
                        if t < 4:
                            if before:
                                weigh(before, 3, t % 4 - 2)
                        elif now:
                            weigh(now, t // 4 - 1, t % 4 - 2)
                    if t == 1 and now:
                        turn_top(it, now, 1, 5)
                    if t == 5 and before:
                        turn_o(it, before, 1, 6)
                    if s := it(1):
                        if t == 6:
                            turn_x4(it, s, 1)
                        if t == 8:
                            project_v(it, s, 1)
                    if t == 9 and maxima:
                        turn_top(it, maxima, 0, 4)
                    if s := it(1):
                        if t == 10:
                            project(it, s, 0, 1)
                        if t == 12:
                            project(it, s, 1, 1)
                    if t == 13 and now:
                        turn_o(it, now, 0, 5)

            pipeline(pe, LAST, body)

        @block.scalar
        def _(act):
            def body(it):
                now, before, maxima, s = it(5), it(6), it(4), it(1)
                for t in range(16):
                    if now:
                        act.wait_ge(products, now.b * 16 + t + 1)
                        if t % 4 == 0 and (t >= 8 or now.after(1)):
                            act.wait_ge(weighed, now.b * 4 + t // 4 - 1)
                        act.activation(p[:, t // 4 % 2, t % 4, :, :], s_ps[:T, t % 2, :, :L], ACT.Exp,
                                       scale=float(D) ** -0.5).then_inc(exps, 1)
                    for at, g, step in ((1, 1, now), (9, 0, maxima)):
                        if t == at and step:
                            act.wait_ge(top_turned, done(step, GROUPS, g + 1))
                            if g or step.after(1):
                                act.wait_ge(top_stored, step.b * 32 + 16 * g)
                            act.copy(top_rows[:, :], misc[:12, :L]).then_inc(top_copied, 1)
                    for at, g, step in ((4, 1, before), (12, 0, now)):
                        if t == at and step:
                            act.wait_ge(weighed, step.b * 4 + 2 * g + 2)
                            if g or step.after(1):
                                act.wait_ge(o_turned, step.b * 2 + g)
                            act.copy(o_t[:, :], o_ps[:, :L]).then_inc(o_copied, 1)
                    if t == 5 and s:
                        act.wait_ge(shift4_ready, done(s))
                        if s.after(1):
                            act.wait_ge(x4t_ready, s.b)
                        for c in range(C):
                            last = act.activation(x4[:, c, :], h[:, bass.ds(tile(s) + c, 1), :].rearrange("p a d -> p (a d)"),
                                                  ACT.Identity, bias=c_shift[:, 0, c:c + 1], scale=c_rstd[:, 0, c:c + 1])
                        last.then_inc(x4_ready, 1)
                    if t == 7 and s:
                        act.wait_ge(x4t_ready, done(s))
                        if s.after(1):
                            act.wait_ge(k_ready, s.b)
                        act.copy(x4_t[:, :], misc[:, :L]).then_inc(x4t_copied, 1)
                    if t == 8 and s:
                        act.wait_ge(v_ready, done(s))
                        if s.after(1):
                            act.wait_ge(parts_there[1 - s.q2], s.b2 * 48 + (48 if s.q2 else 0))
                        act.copy(v_new[:, :, :, 0:DH], misc[:T, :].rearrange("p (c h d) -> p c h d", c=C, h=H)
                                 ).then_inc(v_copied, 1)
                    for at, a, ready, copied in ((10, 0, q_ready, q1_copied), (12, 1, k_ready, k1_copied)):
                        if t == at and s:
                            act.wait_ge(ready, done(s))
                            if s.after(1):
                                act.wait_ge(parts_there[1 - s.q2], s.b2 * 48 + (48 if s.q2 else 0))
                            act.copy(parts[a][:, 0, :], misc[:, :L]).then_inc(copied, 1)
                    if t == 11 and before:
                        act.wait_ge(gain_ready, done(before))
                        if before.after(1):
                            act.wait_ge(res_there, before.b * 16)
                        for c in range(C):
                            last = act.activation(res[:, c, :], h[:, bass.ds(tile(before) + c, 1), :].rearrange("p a d -> p (a d)"),
                                                  ACT.Identity, bias=c_shift[:, 1, c:c + 1], scale=c_gain[:, c:c + 1])
                        last.then_inc(res_ready, 1)

            pipeline(act, LAST, body)

        @block.vector
        def _(dve):
            n = Count(vec_done)
            n.n = vec_from.n

            def maximum(s, head, c):
                at = head * C + c
                dve.wait_ge(scored, s.b * 32 + at + 1)
                if at % 16 == 0 and s.after(1):
                    dve.wait_ge(top_split, done(s, GROUPS, head // 4 + 1) - 2)
                dve.tensor_reduce(top[:, head // 4, head % 4, c:c + 1], max_ps[at % 2][:T, :L], axis=AX.X, op=ALU.max,
                                  negate=True).then_inc(reduced, 1)

            def split_top(s, g):
                dve.wait_ge(reduced, s.b * 32 + 16 * g + 16)
                if s.after(1):
                    dve.wait_ge(top_turned, done(s, GROUPS, g + 1) - 2)
                by_head = top_parts[:, g, :, :, :].rearrange("p c j h -> p j h c")
                got = n.done(dve.tensor_copy(by_head[:, 0, :, :], top[:, g, :, :]))
                dve.wait_ge(vec_done, got)
                got = n.done(dve.tensor_tensor(top_rest[:, :, :], top[:, g, :, :], by_head[:, 0, :, :], ALU.subtract))
                dve.wait_ge(vec_done, got)
                got = n.done(dve.tensor_copy(by_head[:, 1, :, :], top_rest[:, :, :]))
                dve.wait_ge(vec_done, got)
                dve.tensor_tensor(by_head[:, 2, :, :], top_rest[:, :, :], by_head[:, 1, :, :], ALU.subtract).then_inc(top_split, 1)

            def combine(s):
                dve.wait_ge(y_there[s.q2], s.b2 * 128 + 128)
                for k in range(2):
                    got = []
                    for c in range(C):
                        here = h[:, bass.ds(tile(s) + c, 1), :].rearrange("p a d -> p (a d)")
                        if k:
                            dve.wait_ge(vec_done, first[c])
                        ins = dve.scalar_tensor_tensor(
                            out=here, in0=y[:, s.q2, 2 * c + k, :], scalar=share[:, bass.ds(tile(s) + c, 1), k:k + 1],
                            in1=here, op0=ALU.mult, op1=ALU.add)
                        if k == 0 or c < C - 1:
                            got.append(n.done(ins))
                    first = got
                ins.then_inc(combined, 1)
                return got

            def moments_of(s, norm):
                for c in range(C):
                    taken = n.done(dve.bn_stats(c_stats[:, norm, c, :], h[:, bass.ds(tile(s) + c, 1), :]))
                for c in range(C):
                    if c == 0:
                        wait_apart(dve, c_set, vec_done, taken)
                    got = n.done(dve.bn_aggr(c_mom[:, s.q2, norm, c, :], c_stats[:, norm, c, :]))
                dve.wait_ge(vec_done, got)

            def variance(s, norm, ready):
                dve.tensor_scalar(c_var[:, norm, :], c_mom[:, s.q2, norm, :, 1], EPS, None, ALU.add).then_inc(ready, 1)

            def norm_o(s, g):
                dve.wait_ge(o_turned, done(s, GROUPS, g + 1))
                turned = misc[:T, :].rearrange("p (c h e) -> p c h e", c=C, h=4)
                got = n.done(dve.reciprocal(o_inv[:, :, :], turned[:, :, :, DH]))
                dve.wait_ge(vec_done, got)
                if g == 0 and s.after(2):
                    dve.wait_ge(h_done, s.b - 1)
                dve.tensor_tensor(o[:, s.q2, :, :].rearrange("p c (d h) -> p c h d", h=H)[:, :, 4 * g:4 * g + 4, :],
                                  turned[:, :, :, 0:DH], bc(o_inv[:, :, :], 3, DH, [T, C, 4, DH]), ALU.mult).then_inc(o_normed, 1)

            def body(it):
                s, maxima, now, before = it(1), it(4), it(5), it(6)
                for t in range(16):
                    if t == 0 and now:
                        split_top(now, 1)
                    if maxima:
                        maximum(maxima, t // 2, t % 2 * 2)
                        maximum(maxima, t // 2, t % 2 * 2 + 1)
                    if s:
                        if t == 0:
                            combine(s)
                        if t == 1:
                            wait_apart(dve, c_set, combined, done(s))
                            moments_of(s, 0)
                            if s.after(1):
                                dve.wait_ge(rstd4_ready, s.b)
                            variance(s, 0, var4_ready)
                        if t == 3:
                            dve.wait_ge(rstd4_ready, done(s))
                            if s.after(1):
                                dve.wait_ge(x4_ready, s.b)
                            dve.scalar_tensor_tensor(out=c_shift[:, 0, :], in0=c_mom[:, s.q2, 0, :, 0], scalar=-1.0,
                                                     in1=c_rstd[:, 0, :], op0=ALU.mult, op1=ALU.mult).then_inc(shift4_ready, 1)
                        for at, a, ready, rested in ((11, 0, q1_copied, q_rest), (13, 1, k1_copied, k_rest)):
                            if t == at:
                                dve.wait_ge(ready, done(s))
                                if a or s.after(1):
                                    dve.wait_ge(split, s.b * 2 + a)
                                dve.tensor_tensor(rest[:, :], misc[:, :L], parts[a][:, 0, :], ALU.subtract).then_inc(rested, 1)
                    if t == 8 and maxima:
                        split_top(maxima, 0)
                    if before:
                        if t == 6:
                            norm_o(before, 1)
                            dve.wait_ge(o_normed, done(before, 2))
                            here = h[:, bass.ds(tile(before), C), :]
                            dve.tensor_tensor(here, here, o[:, before.q2, :, :], ALU.add).then_inc(h_done, 1)
                        if t == 7:
                            wait_apart(dve, c_set, h_done, done(before))
                            moments_of(before, 1)
                            if before.after(1):
                                dve.wait_ge(rstd5_ready, before.b)
                            variance(before, 1, var5_ready)
                        if t == 10:
                            dve.wait_ge(rstd5_ready, done(before))
                            if before.after(1):
                                dve.wait_ge(res_ready, before.b)
                            n.done(dve.tensor_scalar(c_gain[:, :], c_rstd[:, 1, :], 1.0, None, ALU.add))
                            got = n.now()
                            dve.wait_ge(vec_done, got)
                            dve.scalar_tensor_tensor(out=c_shift[:, 1, :], in0=c_mom[:, before.q2, 1, :, 0], scalar=-1.0,
                                                     in1=c_rstd[:, 1, :], op0=ALU.mult, op1=ALU.mult).then_inc(gain_ready, 1)
                    if t == 15 and now:
                        norm_o(now, 0)

            pipeline(dve, LAST, body, count=n)


_INS = ['x', 'fside_BS_value', 'L0_tok_emb_table', 'L0_tok_w_val', 'L0_tok_b_val', 'L0_tok_gamma_g', 'L0_tok_beta_g',
        'L0_tok_gamma_v', 'L0_tok_beta_v', 'L0_attn_Wg', 'L0_attn_bg', 'L0_attn_Wc', 'L0_attn_bc', 'L0_ffn_gate_w',
        'L0_ffn_w1', 'L0_ffn_w3', 'L0_ffn_w2', 'L0_ffn_sw1', 'L0_ffn_sw3', 'L0_ffn_sw2', 'L1_attn_q_w', 'L1_attn_kv_w']


def kernel(**inputs):
    import numpy as np
    from concourse import bacc
    from concourse.bass_utils import run_bass_kernel_spmd

    nc = bacc.Bacc("TRN2", target_bir_lowering=False, num_devices=1)
    arrays, io = {}, {}
    for name in _INS:
        arrays["in_" + name] = np.ascontiguousarray(inputs[name])
        a = arrays["in_" + name]
        io[name] = nc.dram_tensor("in_" + name, a.shape, mybir.dt.from_np(a.dtype), kind="ExternalInput").ap()
    out = nc.dram_tensor("out_h", (B, L, D), F32, kind="ExternalOutput").ap()
    build(nc, io, out)
    return run_bass_kernel_spmd(nc, [arrays], core_ids=[0]).results[0]["out_h"]
```

```python
from contextlib import ExitStack

import concourse.bass as bass
from concourse import mybir

B, L, D = 32, 500, 128
C, T = 4, 125
NT = B * C
E, CAP, HID = 64, 256, 64
SLOTS = E * CAP
H, DH = 8, 16
EPS = 1e-5
FAR = 65536.0

F32, BF16, I32, U32 = mybir.dt.float32, mybir.dt.bfloat16, mybir.dt.int32, mybir.dt.uint32
ALU = mybir.AluOpType
ACT = mybir.ActivationFunctionType
AX = mybir.AxisListType


class Step:

    def __init__(self, i, reg=None):
        self.q4, self.q2, self.least = i % 4, i % 2, i
        if reg is None:
            self.first = i
            self.b, self.b2, self.b4 = i, i // 2, i // 4
        else:
            self.first = None
            self.b, self.b2, self.b4 = reg * 4 + i, reg * 2 + i // 2, reg + i // 4

    def tile(self):
        return self.b * C

    def after(self, n):
        assert self.first is not None or self.least >= n
        return self.least >= n


class Iteration:

    def __init__(self, i, reg=None):
        self.i, self.reg, self.now = i, reg, Step(i, reg)

    def __call__(self, lag):
        if self.reg is None and not 0 <= self.i - lag < B:
            return None
        return Step(self.i - lag, self.reg)


def pipeline(eng, last, body, count=None, loop_from=8, trips=6):
    per = 0
    for i in range(loop_from):
        at = count.n if count else 0
        body(Iteration(i))
        per = count.n - at if count else 0
    if count:
        count.enter(per * 4)
    with eng.Fori(0, trips) as reg:
        if count:
            count.reg = reg
        for k in range(4):
            body(Iteration(loop_from + k, reg))
    if count:
        count.leave(trips)
    for i in range(loop_from + 4 * trips, last + 1):
        body(Iteration(i))


class Count:

    def __init__(self, sem):
        self.sem, self.n, self.reg, self.per = sem, 0, None, 0

    def enter(self, per):
        self.per, self.at_entry = per, self.n

    def leave(self, trips):
        assert self.n - self.at_entry == self.per, (self.n - self.at_entry, self.per)
        self.n = self.at_entry + self.per * trips
        self.reg, self.per = None, 0

    def now(self):
        return self.reg * self.per + self.n if self.reg is not None else self.n

    def done(self, ins):
        ins.then_inc(self.sem, 1)
        self.n += 1
        return self.now()


def wait_apart(eng, set_up, sem, value):
    if not isinstance(value, int):
        value = eng.to_reg(value)
    eng.wait_ge(set_up, 1)
    eng.wait_ge(sem, value)


def bc(ap, axis, n, shape):
    return ap.unsqueeze(axis).to_broadcast(shape)


def build(nc, io, out):
    top = ExitStack()
    with top:
        def sb(name, shape, dt=F32, ctx=top):
            return ctx.enter_context(nc.sbuf_tensor(name, shape, dt))

        def pb(name, shape, dt=F32, ctx=top):
            return ctx.enter_context(nc.psum_tensor(name, shape, dt))

        keep = {
            "h": sb("h", [T, NT, D]),
            "ident": sb("ident", [128, 128]),
            "w_t": sb("w_t", [128, 6, 128]),
            "top_scores": sb("top_scores", [T, NT, 2]),
            "slots": sb("slots", [T, NT, 2]),
        }
        dram = {
            "x_slots": nc.dram_tensor("x_slots", (SLOTS, D), F32, kind="Internal").ap(),
            "y_slots": nc.dram_tensor("y_slots", (SLOTS, D), F32, kind="Internal").ap(),
            "x_t": nc.dram_tensor("x_t", (B, D, L), F32, kind="Internal").ap(),
        }
        front(nc, io, keep, dram)
        experts(nc, io, keep, dram)
        attention(nc, io, keep, dram, out)


def front(nc, io, keep, dram):
    with ExitStack() as ctx:
        def sb(name, shape, dt=F32):
            return ctx.enter_context(nc.sbuf_tensor(name, shape, dt))

        def pb(name, shape, dt=F32):
            return ctx.enter_context(nc.psum_tensor(name, shape, dt))

        def sem(name):
            return ctx.enter_context(nc.semaphore(name))

        h, ident, w_t = keep["h"], keep["ident"], keep["w_t"]
        w_cv = sb("w_cv", [T, C, D])
        b_cv = sb("b_cv", [T, C, D])
        gamma_g = sb("gamma_g", [T, D])
        beta = sb("beta", [T, D])
        v_scale = sb("v_scale", [T, NT])
        v_rstd = sb("v_rstd", [T, NT])
        ids_t = sb("ids_t", [T, NT], I32)
        bias = sb("bias", [128, 2])
        before = sb("before", [T, T], BF16)
        not_before = sb("not_before", [T, T], BF16)
        ones = sb("ones", [T, T], BF16)
        expert_no = sb("expert_no", [T, E])
        zeros = sb("zeros", [128, 2048])
        eps = sb("eps", [128, 1])
        banks = [pb(f"a_bank{k}", [128, 512]) for k in range(8)]

        ids = sb("ids", [T, 4, C], I32)
        g = sb("g", [T, 4, C, D])
        gn = sb("gn", [T, 2, C, D])
        vn = sb("vn", [T, 2, C, D])
        stats = sb("stats", [T, 3, C, 6])
        moments = sb("moments", [T, 2, 3, C, 2])
        std = sb("std", [T, 2, 3, C])
        rstd = sb("rstd", [T, 2, 3, C])
        shift = sb("shift", [T, 2, 3, C])
        xn = sb("xn", [T, 2, C, D])
        xn_t = sb("xn_t", [D, 2, L])
        hold = sb("hold", [D, 2, L])
        cand = sb("cand", [D, 2, L])
        inflow = sb("inflow", [D, 2, L])
        scan = sb("scan", [D, 2, L])
        x3 = sb("x3", [T, 4, C, D])
        x3_t = sb("x3_t", [D, 2, L])
        top8 = sb("top8", [T, 2, C, 8])
        top_i = sb("top_i", [T, 2, C, 8], U32)
        expert = sb("expert", [T, 2, C, 2])
        hot = sb("hot", [T, 2, C, 2, E], BF16)
        mask = sb("mask", [T, 2, C, E], BF16)
        rank_e = sb("rank_e", [T, C, 2, E])
        pos = sb("pos", [T, C, 2])
        late = sb("late", [T, C, 2])
        slot_0 = sb("slot_0", [T, C, 2])
        slot_i = sb("slot_i", [T, 4, C * 2], I32)
        flag = sb("flag", [1, 1])
        no_mask = sb("no_mask", [T, C * E], BF16)
        xt_ps, gate_ps, cand_ps, scan_ps, x3t_ps, logit_ps, rank_ps = banks[:7]

        gathered = [sem(f"gathered{k}") for k in range(4)]
        scattered = [sem(f"scattered{k}") for k in range(4)]
        x_stored = [sem(f"x_stored{k}") for k in range(2)]
        ids_ready = sem("ids_ready")
        zero_filled = sem("zero_filled")
        stats_ready = sem("stats_ready")
        std_ready = sem("std_ready")
        shift_ready = sem("shift_ready")
        normed = sem("normed")
        values_scaled = sem("values_scaled")
        h_summed = sem("h_summed")
        x_ready = sem("x_ready")
        xt_ready = sem("xt_ready")
        xt_copied = sem("xt_copied")
        gates_ready = sem("gates_ready")
        gates_acted = sem("gates_acted")
        scanned = sem("scanned")
        scan_t_ready = sem("scan_t_ready")
        scan_added = sem("scan_added")
        x3_ready = sem("x3_ready")
        x3t_ready = sem("x3t_ready")
        x3t_copied = sem("x3t_copied")
        logits_ready = sem("logits_ready")
        top_ready = sem("top_ready")
        masked = sem("masked")
        rank_ready = sem("rank_ready")
        rank_read = sem("rank_read")
        pos_ready = sem("pos_ready")
        slot_ready = sem("slot_ready")
        dve_done = sem("dve_done")
        set_up = sem("set_up")
        fill = dram["x_slots"].rearrange("(n p r) d -> n p (r d)", p=128, r=16)
        setup(nc, io, keep, locals())
        block = ctx.enter_context(nc.Block())

        LAST = B + 6

        @block.sync
        def _(sp):
            def body(it):
                if s := it(6):
                    sp.wait_ge(x3t_copied, s.b + 1)
                    sp.dma_start(dram["x_t"][bass.ds(s.b, 1), :, :].rearrange("a d l -> d (a l)"),
                                 x3_t[:, s.q2, :]).then_inc(x_stored[s.q2], 16)

            sp.wait_ge(gathered[3], 64)
            for n in range(SLOTS // 2048):
                sp.dma_start(fill[n, :, :], zeros[:, :]).then_inc(zero_filled, 16)
            pipeline(sp, LAST, body)
            for k in range(2):
                sp.wait_ge(x_stored[k], 16 * B // 2)

        @block.gpsimd
        def _(pool):
            def gather(s):
                if s.after(4):
                    pool.wait_ge(gathered[s.q4], s.b4 * 64)
                    wait_apart(pool, set_up, normed, s.b - 3)
                pool.tensor_copy(ids[:, s.q4, :], ids_t[:, bass.ds(s.tile(), C)]).then_inc(ids_ready, 1)
                wait_apart(pool, set_up, ids_ready, s.b + 1)
                for c in range(C):
                    pool.indirect_dma_start(
                        out=g[:, s.q4, c, :], out_offset=None, in_=io["L0_tok_emb_table"],
                        in_offset=bass.IndirectOffsetOnAxis(ap=ids[:, s.q4, c:c + 1], axis=0),
                    ).then_inc(gathered[s.q4], 16)

            def scatter(s):
                wait_apart(pool, set_up, slot_ready, s.b + 1)
                for j in range(2 * C):
                    pool.indirect_dma_start(
                        out=dram["x_slots"],
                        out_offset=bass.IndirectOffsetOnAxis(ap=slot_i[:, s.q4, j:j + 1], axis=0),
                        in_=x3[:, s.q4, j // 2, :], in_offset=None,
                        bounds_check=SLOTS - 1, oob_is_err=False,
                    ).then_inc(scattered[s.q4], 16)

            def body(it):
                if s := it(0):
                    gather(s)
                if it.i == 7 and it.reg is None:
                    pool.wait_ge(zero_filled, 16 * (SLOTS // 2048))
                if s := it(7):
                    scatter(s)

            pipeline(pool, LAST, body)
            for k in range(4):
                pool.wait_ge(scattered[k], 16 * 2 * C * B // 4)

        @block.scalar
        def _(act):
            def gates(s):
                act.wait_ge(gates_ready, s.b + 1)
                if s.after(2):
                    act.wait_ge(scanned, s.b - 1)
                act.activation(hold[:, s.q2, :], gate_ps[:, :L], ACT.Sigmoid, bias=bias[:, 0:1], scale=-1.0)
                act.activation(cand[:, s.q2, :], cand_ps[:, :L], ACT.Tanh, bias=bias[:, 1:2]).then_inc(gates_acted, 1)

            def scores(s):
                act.wait_ge(top_ready, s.b + 1)
                act.activation(keep["top_scores"][:, bass.ds(s.tile(), C), :], top8[:, s.q2, :, 0:2],
                               ACT.Sigmoid)

            def copy_x3t(s):
                act.wait_ge(x3t_ready, s.b + 1)
                if s.after(2):
                    act.wait_ge(x_stored[s.q2], s.b2 * 16)
                    act.wait_ge(logits_ready, s.b - 1)
                act.copy(x3_t[:, s.q2, :], x3t_ps[:, :L]).then_inc(x3t_copied, 1)

            def copy_xt(s):
                act.wait_ge(xt_ready, s.b + 1)
                if s.after(2):
                    act.wait_ge(gates_ready, s.b - 1)
                act.copy(xn_t[:, s.q2, :], xt_ps[:, :L]).then_inc(xt_copied, 1)

            def norm(now, which, dest, rows, ready):
                for c in range(C):
                    last = act.activation(dest[:, c, :], rows(c), ACT.Identity, bias=shift[:, 1 - now.q2, which, c:c + 1],
                                          scale=rstd[:, 1 - now.q2, which, c:c + 1])
                last.then_inc(ready, 1)

            def h_rows(s):
                return lambda c: h[:, bass.ds(s.tile() + c, 1), :].rearrange("p a d -> p (a d)")

            def scale_values(s):
                if s.after(2):
                    wait_apart(act, set_up, h_summed, s.b - 1)
                for c in range(C):
                    last = act.activation(vn[:, s.q2, c, :], w_cv[:, c, :], ACT.Copy,
                                          scale=v_scale[:, bass.ds(s.tile() + c, 1)])
                last.then_inc(values_scaled, 1)

            def body(it):
                now = it.now
                if now.after(1):
                    wait_apart(act, set_up, shift_ready, now.b)
                if s := it(4):
                    if s.after(2):
                        wait_apart(act, set_up, xt_ready, s.b - 1)
                    norm(now, 1, xn[:, s.q2, :, :], h_rows(s), x_ready)
                if s := it(6):
                    if s.after(4):
                        wait_apart(act, set_up, scattered[s.q4], s.b4 * 16 * 2 * C)
                    norm(now, 2, x3[:, s.q4, :, :], h_rows(s), x3_ready)
                if s := it(4):
                    copy_xt(s)
                if s := it(6):
                    copy_x3t(s)
                if s := it(2):
                    act.wait_ge(gathered[s.q4], s.b4 * 64 + 64)
                    if s.after(2):
                        act.wait_ge(h_summed, s.b - 1)
                    norm(now, 0, gn[:, s.q2, :, :], lambda c: g[:, s.q4, c, :], normed)
                if s := it(1):
                    scale_values(s)
                if s := it(4):
                    gates(s)
                if s := it(7):
                    scores(s)
                act.wait_ge(stats_ready, now.b + 1)
                act.activation(std[:, now.q2, :, :], moments[:, now.q2, :, :, 1], ACT.Sqrt,
                               bias=eps[:T, :]).then_inc(std_ready, 1)

            pipeline(act, LAST, body, loop_from=12, trips=5)

        @block.tensor
        def _(pe):
            pe.matmul(rank_ps[:T, :C * E], ones[:, :], no_mask[:, :], start=True, stop=False, skip_group_check=True)

            def transpose_scan(s):
                pe.wait_ge(scanned, s.b + 1)
                if s.after(1):
                    pe.wait_ge(scan_added, s.b)
                for c in range(C):
                    last = pe.transpose(scan_ps[:T, c * D:(c + 1) * D], scan[:, s.q2, c * T:(c + 1) * T], ident[:, :])
                last.then_inc(scan_t_ready, 1)

            def add_pairs(which, first, past, masks):
                return pe.matmul(rank_ps[:T, first * E:past * E].rearrange("p (c e) -> p c e", e=E), which[:, :],
                                 masks, start=False, stop=False, skip_group_check=True)

            def of_chunk(s, k, times):
                return bc(mask[:, s.q2, k, :], 1, times, [T, times, E])

            def rank(s):
                pe.wait_ge(masked, s.b + 1)
                for k in range(C - 1):
                    add_pairs(ones, k + 1, C, of_chunk(s, k, C - 1 - k))
                add_pairs(before, 0, C, mask[:, s.q2, :, :]).then_inc(rank_ready, 1)

            def count_rest(s):
                pe.wait_ge(rank_read, s.b + 1)
                for k in range(1, C):
                    add_pairs(ones, 0, k, of_chunk(s, k, k))
                add_pairs(not_before, 0, C, mask[:, s.q2, :, :])

            def transpose_x3(s):
                pe.wait_ge(x3_ready, s.b + 1)
                if s.after(1):
                    pe.wait_ge(x3t_copied, s.b)
                for c in range(C):
                    last = pe.transpose(x3t_ps[:, c * T:(c + 1) * T], x3[:, s.q4, c, :], ident[:T, :T])
                last.then_inc(x3t_ready, 1)

            def transpose_x(s):
                pe.wait_ge(x_ready, s.b + 1)
                if s.after(1):
                    pe.wait_ge(xt_copied, s.b)
                for c in range(C):
                    last = pe.transpose(xt_ps[:, c * T:(c + 1) * T], xn[:, s.q2, c, :], ident[:T, :T])
                last.then_inc(xt_ready, 1)

            def logits(s):
                pe.wait_ge(x3t_copied, s.b + 1)
                if s.after(1):
                    pe.wait_ge(masked, s.b)
                for c in range(C):
                    last = pe.matmul(logit_ps[:T, c * D:(c + 1) * D], x3_t[:, s.q2, c * T:(c + 1) * T],
                                     w_t[:, 2, :], start=True, stop=True)
                last.then_inc(logits_ready, 1)

            def gate_products(s):
                pe.wait_ge(xt_copied, s.b + 1)
                if s.after(1):
                    pe.wait_ge(gates_acted, s.b)
                pe.matmul(gate_ps[:, :L], w_t[:, 0, :], xn_t[:, s.q2, :], start=True, stop=True)
                pe.matmul(cand_ps[:, :L], w_t[:, 1, :], xn_t[:, s.q2, :], start=True, stop=True).then_inc(gates_ready, 1)

            def body(it):
                if s := it(4):
                    transpose_x(s)
                if s := it(6):
                    transpose_x3(s)
                if s := it(4):
                    gate_products(s)
                if s := it(5):
                    transpose_scan(s)
                if s := it(7):
                    rank(s)
                if s := it(6):
                    logits(s)
                if s := it(7):
                    count_rest(s)

            pipeline(pe, LAST, body)

        @block.vector
        def _(dve):
            n = Count(dve_done)

            def take_stats(rows, norm):
                for c in range(C):
                    taken = n.done(dve.bn_stats(stats[:, norm, c, :], rows(c)))
                return taken

            def fold_stats(norm, now, taken):
                wait_apart(dve, set_up, dve_done, taken)
                for c in range(C):
                    n.done(dve.bn_aggr(moments[:, now.q2, norm, c, :], stats[:, norm, c, :]))

            def h_rows(s):
                return lambda c: h[:, bass.ds(s.tile() + c, 1), :]

            def scale_rows(s):
                dve.wait_ge(values_scaled, s.b + 1)
                with_beta = n.done(dve.tensor_tensor(vn[:, s.q2, :, :], vn[:, s.q2, :, :],
                                                     bc(beta[:, :], 1, C, [T, C, D]), ALU.add))
                dve.wait_ge(normed, s.b + 1)
                n.done(dve.tensor_tensor(gn[:, s.q2, :, :], gn[:, s.q2, :, :],
                                         bc(gamma_g[:, :], 1, C, [T, C, D]), ALU.mult))
                dve.wait_ge(dve_done, with_beta)
                for c in range(C):
                    scaled = n.done(dve.scalar_tensor_tensor(
                        out=vn[:, s.q2, c, :], in0=b_cv[:, c, :], scalar=v_rstd[:, bass.ds(s.tile() + c, 1)],
                        in1=vn[:, s.q2, c, :], op0=ALU.mult, op1=ALU.add))
                return scaled

            def sum_h(s, scaled):
                dve.wait_ge(dve_done, scaled)
                dve.tensor_tensor(h[:, bass.ds(s.tile(), C), :], gn[:, s.q2, :, :], vn[:, s.q2, :, :],
                                  ALU.add).then_inc(h_summed, 1)

            def flow(s):
                dve.wait_ge(gates_acted, s.b + 1)
                return n.done(dve.scalar_tensor_tensor(out=inflow[:, s.q2, :], in0=hold[:, s.q2, :], scalar=1.0,
                                                       in1=cand[:, s.q2, :], op0=ALU.subtract, op1=ALU.mult))

            def scan_gates(s, flown):
                dve.wait_ge(dve_done, flown)
                if s.after(2):
                    dve.wait_ge(scan_t_ready, s.b - 1)
                dve.tensor_tensor_scan(out=scan[:, s.q2, :], data0=hold[:, s.q2, :], data1=inflow[:, s.q2, :],
                                       initial=0.0, op0=ALU.mult, op1=ALU.add).then_inc(scanned, 1)

            def add_scan(s):
                dve.wait_ge(scan_t_ready, s.b + 1)
                here = h[:, bass.ds(s.tile(), C), :]
                dve.tensor_tensor(here, here, scan_ps[:T, :C * D].rearrange("p (c d) -> p c d", c=C),
                                  ALU.subtract).then_inc(scan_added, 1)

            def top_two(s):
                wait_apart(dve, set_up, logits_ready, s.b + 1)
                for c in range(C):
                    top = dve.max(out=top8[:, s.q2, c, :], in_=logit_ps[:T, c * D:c * D + E])
                    if c < C - 1:
                        n.done(top)
                top.then_inc(top_ready, 1)

            def top_experts(s):
                wait_apart(dve, set_up, top_ready, s.b + 1)
                for c in range(C):
                    placed = n.done(dve.max_index(out=top_i[:, s.q2, c, :], in_max=top8[:, s.q2, c, :],
                                                  in_values=logit_ps[:T, c * D:c * D + E]))
                return placed

            def experts_as_floats(s, placed):
                dve.wait_ge(dve_done, placed)
                return n.done(dve.tensor_copy(expert[:, s.q2, :, :], top_i[:, s.q2, :, 0:2]))

            def route(s, known):
                dve.wait_ge(dve_done, known)
                lit = n.done(dve.tensor_tensor(
                    hot[:, s.q2, :, :, :].rearrange("p c k e -> p (c k) e"),
                    bc(expert_no[:, :], 1, 2 * C, [T, 2 * C, E]),
                    bc(expert[:, s.q2, :, :].rearrange("p c k -> p (c k)"), 2, E, [T, 2 * C, E]), ALU.is_equal))
                dve.wait_ge(dve_done, lit)
                dve.tensor_tensor(mask[:, s.q2, :, :], hot[:, s.q2, :, 0, :], hot[:, s.q2, :, 1, :],
                                  ALU.add).then_inc(masked, 1)

            def read_rank(s):
                dve.wait_ge(rank_ready, s.b + 1)
                dve.tensor_tensor(rank_e[:, :, :, :], hot[:, s.q2, :, :, :],
                                  bc(rank_ps[:T, :C * E].rearrange("p (c e) -> p c e", c=C), 2, 2, [T, C, 2, E]),
                                  ALU.mult).then_inc(rank_read, 1)

            def sum_rank(s):
                dve.wait_ge(rank_read, s.b + 1)
                dve.tensor_reduce(pos[:, :, :], rank_e[:, :, :, :], axis=AX.X, op=ALU.add).then_inc(pos_ready, 1)

            def place(s):
                dve.wait_ge(pos_ready, s.b + 1)
                n.done(dve.tensor_scalar(late[:, :, :], pos[:, :, :], float(CAP), FAR, ALU.is_ge, ALU.mult))
                both = n.done(dve.scalar_tensor_tensor(out=slot_0[:, :, :], in0=expert[:, s.q2, :, :], scalar=float(CAP),
                                                       in1=pos[:, :, :], op0=ALU.mult, op1=ALU.add))
                dve.wait_ge(dve_done, both)
                slots = keep["slots"][:, bass.ds(s.tile(), C), :]
                put = n.done(dve.tensor_tensor(slots, slot_0[:, :, :], late[:, :, :], ALU.add))
                wait_apart(dve, set_up, dve_done, put)
                dve.tensor_copy(slot_i[:, s.q4, :].rearrange("p (c k) -> p c k", c=C), slots).then_inc(slot_ready, 1)

            def body(it):
                now, rows, summed, scanning, routed = it.now, it(1), it(3), it(5), it(7)
                if summed:
                    scaled = scale_rows(summed)
                if rows:
                    dve.wait_ge(gathered[rows.q4], rows.b4 * 64 + 64)
                    taken = take_stats(lambda c: g[:, rows.q4, c, :], 0)
                if summed:
                    sum_h(summed, scaled)
                if rows:
                    fold_stats(0, now, taken)
                if summed:
                    wait_apart(dve, set_up, h_summed, summed.b + 1)
                    taken = take_stats(h_rows(summed), 1)
                if routed:
                    top_two(routed)
                if summed:
                    fold_stats(1, now, taken)
                if routed:
                    placed = top_experts(routed)
                if scanning:
                    flown = flow(scanning)
                if routed:
                    known = experts_as_floats(routed, placed)
                if scanning:
                    scan_gates(scanning, flown)
                if routed:
                    route(routed, known)
                if scanning:
                    add_scan(scanning)
                if routed:
                    read_rank(routed)
                if scanning:
                    wait_apart(dve, set_up, scan_added, scanning.b + 1)
                    taken = take_stats(h_rows(scanning), 2)
                if routed:
                    sum_rank(routed)
                if scanning:
                    fold_stats(2, now, taken)
                dve.wait_ge(dve_done, n.now())
                dve.memset(flag[:, :], 0.0).then_inc(stats_ready, 1)
                if routed:
                    place(routed)
                dve.wait_ge(std_ready, now.b + 1)
                got = n.done(dve.reciprocal(rstd[:, now.q2, :, :], std[:, now.q2, :, :]))
                dve.wait_ge(dve_done, got)
                dve.scalar_tensor_tensor(out=shift[:, now.q2, :, :], in0=moments[:, now.q2, :, :, 0], scalar=-1.0,
                                         in1=rstd[:, now.q2, :, :], op0=ALU.mult, op1=ALU.mult).then_inc(shift_ready, 1)

            pipeline(dve, LAST, body, count=n)


def setup(nc, io, keep, own):
    with ExitStack() as ctx:
        def sb(name, shape, dt=F32):
            return ctx.enter_context(nc.sbuf_tensor(name, shape, dt))

        def sem(name):
            return ctx.enter_context(nc.semaphore(name))

        ident, w_t = keep["ident"], keep["w_t"]
        w_cv, b_cv, beta, gamma_g = own["w_cv"], own["b_cv"], own["beta"], own["gamma_g"]
        v_scale, v_rstd, ids_t, bias, banks = (own[k] for k in ("v_scale", "v_rstd", "ids_t", "bias", "banks"))
        raw = sb("raw", [128, 6, 128])
        ids_i = sb("ids_i", [NT, T], I32)
        ids_f = sb("ids_f", [NT, T])
        value = sb("value", [NT, T])
        value_t = sb("value_t", [T, NT])
        wv = sb("wv", [T, C, D])
        bv = sb("bv", [T, C, D])
        gamma_v = sb("gamma_v", [T, D])
        betas = sb("betas", [T, 2, D])
        cross = sb("cross", [T, C, D])
        st = sb("st", [T, 2, C, 6])
        mv = sb("mv", [T, 2, C, 2])
        cov = sb("cov", [T, C])
        var = sb("var", [T, NT])
        term = sb("term", [T, NT])
        square = sb("square", [T, NT])
        loaded, values_loaded, made, transposed, copied, done, rooted, var_ready = (sem(n) for n in (
            "loaded", "values_loaded", "made", "transposed", "copied", "done", "rooted", "var_ready"))
        weights = [(io["L0_attn_Wg"], 128), (io["L0_attn_Wc"], 128), (io["L0_ffn_gate_w"], E), (io["L1_attn_q_w"], 128),
                   (io["L1_attn_kv_w"][0:128, :], 128), (io["L1_attn_kv_w"][128:256, :], 128)]
        block = ctx.enter_context(nc.Block())

        @block.sync
        def _(sp):
            sp.dma_start(ids_i[:, :], io["x"].rearrange("b (c p) -> (b c) p", c=C)).then_inc(values_loaded, 16)
            sp.dma_start(value[:, :], io["fside_BS_value"].rearrange("b (c p) -> (b c) p", c=C)).then_inc(values_loaded, 16)
            sp.dma_start(wv[:, :, :], io["L0_tok_w_val"].rearrange("(c p) d -> p c d", c=C)).then_inc(values_loaded, 16)
            sp.dma_start(bv[:, :, :], io["L0_tok_b_val"].rearrange("(c p) d -> p c d", c=C)).then_inc(values_loaded, 16)
            for dest, name in ((gamma_v[:, :], "L0_tok_gamma_v"), (gamma_g[:, :], "L0_tok_gamma_g"),
                               (betas[:, 0, :], "L0_tok_beta_g"), (betas[:, 1, :], "L0_tok_beta_v")):
                sp.dma_start(dest, io[name].partition_broadcast(T)).then_inc(values_loaded, 16)
            for k, (w, rows) in enumerate(weights):
                sp.dma_start(raw[:rows, k, :], w).then_inc(loaded, 16)
            sp.dma_start(bias[:, 0:1], io["L0_attn_bg"].rearrange("(p a) -> p a", a=1)).then_inc(loaded, 16)
            sp.dma_start(bias[:, 1:2], io["L0_attn_bc"].rearrange("(p a) -> p a", a=1)).then_inc(loaded, 16)

        @block.gpsimd
        def _(pool):
            pool.memset(own["zeros"][:, :], 0.0).then_inc(made, 1)
            pool.memset(own["flag"][:, :], 0.0).then_inc(own["set_up"], 1)
            pool.memset(ident[:, :], 0.0).then_inc(made, 1)
            pool.memset(own["ones"][:, :], 1.0).then_inc(made, 1)
            pool.memset(own["before"][:, :], 1.0).then_inc(made, 1)
            pool.memset(own["not_before"][:, :], 1.0).then_inc(made, 1)
            pool.wait_ge(made, 5)
            pool.affine_select(out=ident[:, :], in_=ident[:, :], compare_op=ALU.not_equal, fill=1.0,
                               base=0, pattern=[[-1, 128]], channel_multiplier=1).then_inc(made, 1)
            pool.affine_select(out=own["before"][:, :], in_=own["before"][:, :], compare_op=ALU.is_gt, fill=0.0,
                               base=0, pattern=[[1, T]], channel_multiplier=-1).then_inc(made, 1)
            pool.affine_select(out=own["not_before"][:, :], in_=own["not_before"][:, :], compare_op=ALU.is_ge, fill=0.0,
                               base=0, pattern=[[-1, T]], channel_multiplier=1).then_inc(made, 1)
            pool.iota(own["expert_no"][:, :], pattern=[[1, E]], base=0, channel_multiplier=0,
                      allow_small_or_imprecise_dtypes=True).then_inc(made, 1)
            pool.memset(w_t[:, 2, E:], 0.0).then_inc(made, 1)
            pool.memset(own["eps"][:, :], EPS).then_inc(made, 1)
            pool.memset(own["moments"][:, :, :, :, :], 1.0).then_inc(made, 1)
            pool.memset(own["no_mask"][:, :], 0.0).then_inc(made, 1)
            pool.wait_ge(made, 13)

        @block.tensor
        def _(pe):
            pe.wait_ge(made, 6)
            pe.wait_ge(loaded, 16 * 8)
            for k, (_, rows) in enumerate(weights):
                pe.transpose(banks[k][:, :rows], raw[:rows, k, :], ident[:rows, :rows]).then_inc(transposed, 1)
            pe.wait_ge(copied, 1)
            pe.transpose(banks[6][:T, :NT], ids_f[:, :], ident[:, :]).then_inc(transposed, 1)
            pe.transpose(banks[7][:T, :NT], value[:, :], ident[:, :]).then_inc(transposed, 1)

        @block.scalar
        def _(act):
            act.wait_ge(var_ready, 1)
            act.wait_ge(made, 13)
            act.activation(var[:, :], var[:, :], ACT.Sqrt, bias=own["eps"][:T, :]).then_inc(rooted, 1)

        @block.vector
        def _(dve):
            n = Count(done)

            def link(ins):
                dve.wait_ge(done, n.done(ins))

            dve.wait_ge(values_loaded, 16 * 8)
            dve.tensor_copy(ids_f[:, :], ids_i[:, :]).then_inc(copied, 1)
            for c in range(C):
                n.done(dve.bn_stats(st[:, 0, c, :], wv[:, c, :]))
                link(dve.bn_stats(st[:, 1, c, :], bv[:, c, :]))
            for c in range(C):
                n.done(dve.bn_aggr(mv[:, 0, c, :], st[:, 0, c, :]))
                link(dve.bn_aggr(mv[:, 1, c, :], st[:, 1, c, :]))
            n.done(dve.tensor_tensor(wv[:, :, :], wv[:, :, :], mv[:, 0, :, 0:1].to_broadcast([T, C, D]), ALU.subtract))
            link(dve.tensor_tensor(bv[:, :, :], bv[:, :, :], mv[:, 1, :, 0:1].to_broadcast([T, C, D]), ALU.subtract))
            link(dve.tensor_tensor(cross[:, :, :], wv[:, :, :], bv[:, :, :], ALU.mult))
            link(dve.tensor_reduce(cov[:, :], cross[:, :, :], axis=AX.X, op=ALU.add))
            gv = bc(gamma_v[:, :], 1, C, [T, C, D])
            n.done(dve.tensor_tensor(w_cv[:, :, :], wv[:, :, :], gv, ALU.mult))
            n.done(dve.tensor_tensor(b_cv[:, :, :], bv[:, :, :], gv, ALU.mult))
            n.done(dve.tensor_tensor(beta[:, :], betas[:, 0, :], betas[:, 1, :], ALU.add))
            dve.wait_ge(transposed, 8)
            n.done(dve.tensor_copy(ids_t[:, :], banks[6][:T, :NT]))
            link(dve.tensor_copy(value_t[:, :], banks[7][:T, :NT]))

            def by_chunk(x):
                return x.rearrange("p (b c) -> p b c", c=C)

            def over_batches(x):
                return bc(x, 1, B, [T, B, C])

            link(dve.tensor_tensor(square[:, :], value_t[:, :], value_t[:, :], ALU.mult))
            n.done(dve.tensor_tensor(by_chunk(square[:, :]), by_chunk(square[:, :]), over_batches(mv[:, 0, :, 1]), ALU.mult))
            link(dve.tensor_tensor(by_chunk(term[:, :]), by_chunk(value_t[:, :]), over_batches(cov[:, :]), ALU.mult))
            link(dve.scalar_tensor_tensor(out=var[:, :], in0=term[:, :], scalar=2.0 / D, in1=square[:, :],
                                          op0=ALU.mult, op1=ALU.add))
            link(dve.tensor_tensor(by_chunk(var[:, :]), by_chunk(var[:, :]), over_batches(mv[:, 1, :, 1]), ALU.add))
            dve.tensor_scalar(var[:, :], var[:, :], 0.0, None, ALU.max).then_inc(var_ready, 1)
            for k, (_, rows) in enumerate(weights):
                n.done(dve.tensor_copy(w_t[:, k, :rows], banks[k][:, :rows]))
            dve.wait_ge(loaded, 16 * 8)
            n.done(dve.tensor_scalar(bias[:, 0:1], bias[:, 0:1], -1.0, None, ALU.mult))
            dve.wait_ge(rooted, 1)
            link(dve.reciprocal(v_rstd[:, :], var[:, :]))
            link(dve.tensor_tensor(v_scale[:, :], value_t[:, :], v_rstd[:, :], ALU.mult))


def experts(nc, io, keep, dram):
    with ExitStack() as ctx:
        def sb(name, shape, dt=F32):
            return ctx.enter_context(nc.sbuf_tensor(name, shape, dt))

        def sem(name):
            return ctx.enter_context(nc.semaphore(name))

        h = keep["h"]
        shared = sb("shared", [D, 3, D])
        xt = sb("xt", [D, 4, L])
        xs = sb("xs", [128, 4, 4, D])
        xst = sb("xst", [D, 2, 4 * 128])
        w1 = sb("w1", [D, 4, 2, HID])
        w3 = sb("w3", [D, 4, 2, HID])
        w2 = sb("w2", [2 * HID, 4, D])
        s_sig = sb("s_sig", [D, 2, L])
        s_hid = sb("s_hid", [D, 2, L])
        e_sig = sb("e_sig", [2 * HID, 2, CAP])
        e_hid = sb("e_hid", [2 * HID, 2, CAP])
        y = sb("y", [128, 2, 4, D])
        banks = [ctx.enter_context(nc.psum_tensor(f"b_bank{k}", [128, 512], F32)) for k in range(5)]
        xst_ps, s1_ps, s3_ps, hid_ps, sum_ps = banks
        y_ps = ctx.enter_context(nc.psum_tensor("y_ps", [128, 2, 512], F32))
        loaded = [sem(f"e_loaded{k}") for k in range(4)]
        y_stored = [sem(f"y_stored{k}") for k in range(2)]
        (shared_loaded, slots_turned, turned_copied, shared_up, s_sig_ready, s_silu, s_hid_ready, hidden_up, e_sig_ready,
         e_silu, e_hid_ready, shared_down, shared_added, y_ready, y_copied) = (sem(k) for k in (
            "shared_loaded slots_turned turned_copied shared_up s_sig_ready s_silu s_hid_ready hidden_up e_sig_ready "
            "e_silu e_hid_ready shared_down shared_added y_ready y_copied").split())
        block = ctx.enter_context(nc.Block())
        LAST = B + 4

        @block.sync
        def _(sp):
            for k, name in enumerate(("L0_ffn_sw1", "L0_ffn_sw3", "L0_ffn_sw2")):
                sp.dma_start(shared[:, k, :], io[name]).then_inc(shared_loaded, 16)
            x_slots = dram["x_slots"].rearrange("(j u p) d -> j p u d", u=4, p=128)
            y_slots = dram["y_slots"].rearrange("(j u p) d -> j p u d", u=4, p=128)
            w1_pairs = io["L0_ffn_w1"].rearrange("(j e) d h -> j d e h", e=2)
            w3_pairs = io["L0_ffn_w3"].rearrange("(j e) d h -> j d e h", e=2)
            w2_pairs = io["L0_ffn_w2"].rearrange("(j e) h d -> j (e h) d", e=2)

            def pair(x, s, pattern="j p u d -> p (j u) d"):
                return x[bass.ds(s.b, 1)].rearrange(pattern)

            def load(s):
                if s.after(4):
                    sp.wait_ge(y_ready, s.b - 3)
                    sp.wait_ge(shared_up, s.b - 3)
                into = loaded[s.q4]
                sp.dma_start(xs[:, s.q4, :, :], pair(x_slots, s)).then_inc(into, 16)
                sp.dma_start(xt[:, s.q4, :], pair(dram["x_t"], s, "j d l -> d (j l)")).then_inc(into, 16)
                sp.dma_start(w1[:, s.q4, :, :], pair(w1_pairs, s)).then_inc(into, 16)
                sp.dma_start(w3[:, s.q4, :, :], pair(w3_pairs, s)).then_inc(into, 16)
                sp.dma_start(w2[:, s.q4, :], pair(w2_pairs, s, "j r d -> r (j d)")).then_inc(into, 16)

            def store(s):
                sp.wait_ge(y_copied, s.b + 1)
                sp.dma_start(pair(y_slots, s), y[:, s.q2, :, :]).then_inc(y_stored[s.q2], 16)

            def body(it):
                if s := it(0):
                    load(s)
                if s := it(5):
                    store(s)

            pipeline(sp, LAST, body)
            for k in range(2):
                sp.wait_ge(y_stored[k], 16 * B // 2)

        @block.tensor
        def _(pe):
            pe.wait_ge(shared_loaded, 48)

            def turn_slots(s):
                pe.wait_ge(loaded[s.q4], s.b4 * 80 + 80)
                if s.after(1):
                    pe.wait_ge(turned_copied, s.b)
                for u in range(4):
                    last = pe.transpose(xst_ps[:, u * 128:(u + 1) * 128], xs[:, s.q4, u, :], keep["ident"][:, :])
                last.then_inc(slots_turned, 1)

            def up_shared(s):
                if s.after(1):
                    pe.wait_ge(s_hid_ready, s.b)
                pe.matmul(s1_ps[:, :L], shared[:, 0, :], xt[:, s.q4, :], start=True, stop=True)
                pe.matmul(s3_ps[:, :L], shared[:, 1, :], xt[:, s.q4, :], start=True, stop=True).then_inc(shared_up, 1)

            def up_experts(s):
                pe.wait_ge(turned_copied, s.b + 1)
                if s.after(1):
                    pe.wait_ge(e_hid_ready, s.b)
                for half, w in ((0, w1), (1, w3)):
                    for e in range(2):
                        last = pe.matmul(hid_ps[e * HID:(e + 1) * HID, half * CAP:(half + 1) * CAP], w[:, s.q4, e, :],
                                         xst[:, s.q2, e * CAP:(e + 1) * CAP], start=True, stop=True)
                last.then_inc(hidden_up, 1)

            def down_shared(s):
                pe.wait_ge(s_hid_ready, s.b + 1)
                if s.after(1):
                    pe.wait_ge(shared_added, s.b)
                for c in range(C):
                    last = pe.matmul(sum_ps[:T, c * D:(c + 1) * D], s_hid[:, s.q2, c * T:(c + 1) * T], shared[:, 2, :],
                                     start=True, stop=True)
                last.then_inc(shared_down, 1)

            def down_experts(s):
                pe.wait_ge(e_hid_ready, s.b + 1)
                if s.after(1):
                    pe.wait_ge(y_copied, s.b)
                for u in range(4):
                    rows = slice(u // 2 * HID, (u // 2 + 1) * HID)
                    last = pe.matmul(y_ps[:, u // 2, u % 2 * D:(u % 2 + 1) * D], e_hid[rows, s.q2, u % 2 * 128:(u % 2 + 1) * 128],
                                     w2[rows, s.q4, :], start=True, stop=True)
                last.then_inc(y_ready, 1)

            def body(it):
                if s := it(3):
                    turn_slots(s)
                    up_shared(s)
                if s := it(4):
                    down_shared(s)
                if s := it(3):
                    up_experts(s)
                if s := it(4):
                    down_experts(s)

            pipeline(pe, LAST, body)

        @block.scalar
        def _(act):
            def body(it):
                if s := it(3):
                    act.wait_ge(slots_turned, s.b + 1)
                    if s.after(2):
                        act.wait_ge(hidden_up, s.b - 1)
                    act.copy(xst[:, s.q2, :], xst_ps[:, :]).then_inc(turned_copied, 1)
                    act.wait_ge(shared_up, s.b + 1)
                    if s.after(2):
                        act.wait_ge(s_silu, s.b - 1)
                    act.activation(s_sig[:, s.q2, :], s1_ps[:, :L], ACT.Sigmoid).then_inc(s_sig_ready, 1)
                    act.wait_ge(hidden_up, s.b + 1)
                    if s.after(2):
                        act.wait_ge(e_silu, s.b - 1)
                    act.activation(e_sig[:, s.q2, :], hid_ps[:, :CAP], ACT.Sigmoid).then_inc(e_sig_ready, 1)
                if s := it(4):
                    act.wait_ge(y_ready, s.b + 1)
                    if s.after(2):
                        act.wait_ge(y_stored[s.q2], s.b2 * 16)
                    act.copy(y[:, s.q2, :, :].rearrange("p (e u) d -> p e (u d)", e=2),
                             y_ps[:, :, :2 * D]).then_inc(y_copied, 1)

            pipeline(act, LAST, body)

        @block.vector
        def _(dve):
            def body(it):
                if s := it(3):
                    dve.wait_ge(s_sig_ready, s.b + 1)
                    if s.after(2):
                        dve.wait_ge(shared_down, s.b - 1)
                    dve.tensor_tensor(s_hid[:, s.q2, :], s_sig[:, s.q2, :], s1_ps[:, :L], ALU.mult).then_inc(s_silu, 1)
                    dve.wait_ge(s_silu, s.b + 1)
                    dve.tensor_tensor(s_hid[:, s.q2, :], s_hid[:, s.q2, :], s3_ps[:, :L], ALU.mult).then_inc(s_hid_ready, 1)
                    dve.wait_ge(e_sig_ready, s.b + 1)
                    if s.after(2):
                        dve.wait_ge(y_ready, s.b - 1)
                    dve.tensor_tensor(e_hid[:, s.q2, :], e_sig[:, s.q2, :], hid_ps[:, :CAP], ALU.mult).then_inc(e_silu, 1)
                    dve.wait_ge(e_silu, s.b + 1)
                    dve.tensor_tensor(e_hid[:, s.q2, :], e_hid[:, s.q2, :], hid_ps[:, CAP:], ALU.mult).then_inc(e_hid_ready, 1)
                if s := it(4):
                    dve.wait_ge(shared_down, s.b + 1)
                    here = h[:, bass.ds(s.tile(), C), :]
                    dve.tensor_tensor(here, here, sum_ps[:T, :].rearrange("p (c d) -> p c d", c=C),
                                      ALU.add).then_inc(shared_added, 1)

            pipeline(dve, LAST, body)


NROW = 6 * DH
SROW = NROW + 3


def attention(nc, io, keep, dram, out):
    with ExitStack() as ctx:
        def sb(name, shape, dt=F32):
            return ctx.enter_context(nc.sbuf_tensor(name, shape, dt))

        def pb(name, shape, dt=F32):
            return ctx.enter_context(nc.psum_tensor(name, shape, dt))

        def sem(name):
            return ctx.enter_context(nc.semaphore(name))

        h, ident, w_t, slots = keep["h"], keep["ident"], keep["w_t"], keep["slots"]
        share = sb("share", [T, NT, 2])
        slots_i = sb("slots_i", [T, NT, 2], I32)
        total = sb("total", [T, NT])
        qk_w = sb("qk_w", [D, 2, D])
        v_new = sb("v_new", [T, C, H, DH + 1])
        identb = sb("identb", [T, T], BF16)
        minus_half = sb("minus_half", [T, C])
        q_st = sb("q_st", [SROW, 4, H, L], BF16)
        k_st = sb("k_st", [SROW, 4, H, L], BF16)
        v = sb("v", [T, 4, C, H, DH + 1])
        y_idx = sb("y_idx", [T, 2, C * 2], I32)
        y = sb("y_pairs", [T, 2, C * 2, D])
        c_stats = sb("c_stats", [T, 2, C, 6])
        c_mom = sb("c_mom", [T, 2, 2, C, 2])
        c_var = sb("c_var", [T, 2, C])
        c_rstd = sb("c_rstd", [T, 2, C])
        c_gain = sb("c_gain", [T, C])
        c_shift = sb("c_shift", [T, 2, C])
        x4 = sb("x4", [T, C, D])
        x4_t = sb("x4_t", [D, L])
        parts = [sb(f"{a}_parts", [D, 3, L], BF16) for a in "qk"]
        rest = sb("rest", [D, L])
        top = sb("top", [T, 2, 4, C])
        top_rest = sb("top_rest", [T, 4, C])
        top_parts = sb("top_parts", [T, 2, C, 3, 4], BF16)
        top_rows = sb("top_rows", [12, L], BF16)
        one_row = top_rows[:SROW - NROW, :]
        p = sb("p", [T, 2, 4, 2, L])
        o_t = sb("o_t", [128, L])
        o_inv = sb("o_inv", [T, C, 4])
        o = sb("o", [T, 2, C, D])
        res = sb("res", [T, C, D])

        max_ps = pb("max_ps", [128, 2, 2, 512])
        s_ps = pb("s_ps", [128, 2, 512])
        o_ps = pb("o_ps", [128, 512])
        misc = pb("misc", [128, 512])

        parts_d = [nc.dram_tensor(f"{a}_parts_d", (2, 3, D, L), BF16, kind="Internal").ap() for a in "qk"]
        v_d = nc.dram_tensor("v_d", (2, T, C * H * (DH + 1)), F32, kind="Internal").ap()
        top_d = nc.dram_tensor("top_d", (2, 12, L), BF16, kind="Internal").ap()

        y_there = [sem(f"y_there{k}") for k in range(2)]
        stacked = [sem(f"stacked{k}") for k in range(4)]
        parts_there = [[sem(f"{a}_parts_there{k}") for k in range(2)] for a in "qk"]
        v_there = sem("v_there")
        one_row_set = sem("one_row_set")
        ones_there = sem("ones_there")
        res_there = sem("res_there")
        top_stored = sem("top_stored")
        top_there = [sem(f"top_there{k}") for k in range(2)]
        (c_set, idx_ready, var4_ready, rstd4_ready, shift4_ready, x4_ready, x4t_ready, x4t_copied, v_ready, v_copied,
         q_ready, q1_copied, q_rest, k_ready, k1_copied, k_rest, split, scored, reduced, top_split, top_turned,
         top_copied, products, exps, weighed, o_copied, o_turned, o_normed, h_done, var5_ready, rstd5_ready, gain_ready,
         res_ready, vec_done, pool_done, first_added, second_scaled, combined) = (sem("c_" + k) for k in (
            "c_set idx_ready var4_ready rstd4_ready shift4_ready x4_ready x4t_ready x4t_copied v_ready v_copied "
            "q_ready q1_copied q_rest k_ready k1_copied k_rest split scored reduced top_split top_turned "
            "top_copied products exps weighed o_copied o_turned o_normed h_done var5_ready rstd5_ready gain_ready "
            "res_ready vec_done pool_done first_added second_scaled combined").split())

        def tile(s):
            return s.b2 * C + s.q2 * (NT // 2)

        def done(s, per=1, of=0):
            return s.b * per + (of or per)

        vec_from, pool_from = Count(vec_done), 3
        with nc.Block() as block:
            @block.gpsimd
            def _(pool):
                pool.memset(one_row[:, :], 1.0).then_inc(one_row_set, 1)
                pool.memset(minus_half[:, :], -0.5).then_inc(pool_done, 1)
                pool.memset(y[:, :, :, :], 0.0).then_inc(pool_done, 1)
                pool.memset(v_new[:, :, :, :], 1.0).then_inc(pool_done, 1)
                pool.wait_ge(pool_done, 3)

            @block.sync
            def _(sp):
                sp.wait_ge(one_row_set, 1)
                sp.dma_start(k_st[NROW:SROW, :, :, :].rearrange("r s h n -> r (s h) n"),
                             bc(one_row[:, :], 1, 4 * H, [SROW - NROW, 4 * H, L])).then_inc(ones_there, 16)
                sp.wait_ge(ones_there, 16)

            @block.scalar
            def _(act):
                act.copy(identb[:, :], ident[:T, :T]).then_inc(c_set, 1)

            @block.vector
            def _(dve):
                n = vec_from

                def link(ins):
                    dve.wait_ge(vec_done, n.done(ins))

                score = keep["top_scores"]
                n.done(dve.memset(o_ps[:, :], 0.0))
                for a in range(2):
                    n.done(dve.tensor_copy(qk_w[:, a, :].rearrange("p (d h) -> p d h", h=H),
                                           w_t[:, 3 + a, :].rearrange("p (h d) -> p d h", h=H)))
                n.done(dve.tensor_copy(slots_i[:, :, :], slots[:, :, :]))
                link(dve.tensor_tensor(total[:, :], score[:, :, 0], score[:, :, 1], ALU.add))
                link(dve.tensor_scalar(total[:, :], total[:, :], 1e-20, None, ALU.add))
                link(dve.reciprocal(total[:, :], total[:, :]))
                link(dve.tensor_tensor(share[:, :, :], score[:, :, :], bc(total[:, :], 2, 2, [T, NT, 2]), ALU.mult))
                link(dve.tensor_scalar(slots[:, :, :], slots[:, :, :], float(SLOTS), 2.5, ALU.is_lt, ALU.mult))
                link(dve.tensor_tensor(share[:, :, :], share[:, :, :], slots[:, :, :], ALU.mult))

        block = ctx.enter_context(nc.Block())
        LAST = B + 6
        GROUPS = 2

        @block.gpsimd
        def _(pool):
            n = Count(pool_done)
            n.n = pool_from

            def gather(s, half):
                if half == 0:
                    if s.after(2):
                        pool.wait_ge(combined, s.b - 1)
                        pool.wait_ge(y_there[s.q2], s.b2 * 128)
                    pool.tensor_copy(y_idx[:, s.q2, :].rearrange("p (c k) -> p c k", k=2),
                                     slots_i[:, bass.ds(tile(s), C), :]).then_inc(idx_ready, 1)
                    wait_apart(pool, c_set, idx_ready, done(s))
                for j in range(half * C, half * C + C):
                    pool.indirect_dma_start(
                        out=y[:, s.q2, j, :], out_offset=None, in_=dram["y_slots"],
                        in_offset=bass.IndirectOffsetOnAxis(ap=y_idx[:, s.q2, j:j + 1], axis=0),
                        bounds_check=SLOTS - 1, oob_is_err=False,
                    ).then_inc(y_there[s.q2], 16)

            def root(s, ready, norm, into):
                pool.wait_ge(ready, done(s))
                pool.tensor_tensor(c_rstd[:, norm, :], c_var[:, norm, :], minus_half[:, :], ALU.pow).then_inc(into, 1)

            def split_rest(s, a, ready):
                wait_apart(pool, c_set, ready, done(s))
                second = n.done(pool.tensor_copy(parts[a][:, 1, :], rest[:, :]))
                pool.wait_ge(pool_done, second)
                pool.tensor_tensor(parts[a][:, 2, :], rest[:, :], parts[a][:, 1, :], ALU.subtract).then_inc(split, 1)

            def add_second(s):
                wait_apart(pool, c_set, first_added, done(s))
                wait_apart(pool, c_set, second_scaled, done(s))
                here = h[:, bass.ds(tile(s), C), :]
                pool.tensor_tensor(here, here, y[:, s.q2, :, :].rearrange("p (c k) d -> p c k d", k=2)[:, :, 1, :],
                                   ALU.add).then_inc(combined, 1)

            def add_o(s):
                wait_apart(pool, c_set, o_normed, done(s, 2))
                here = h[:, bass.ds(tile(s), C), :]
                pool.tensor_tensor(here, here, o[:, s.q2, :, :], ALU.add).then_inc(h_done, 1)

            def body(it):
                early = it.reg is None and it.i == 3
                if (s := it(0)) and not early:
                    gather(s, 0)
                if s := it(1):
                    add_second(s)
                if s := it(2):
                    split_rest(s, 0, q_rest)
                if s := it(1):
                    root(s, var4_ready, 0, rstd4_ready)
                if s := it(2):
                    split_rest(s, 1, k_rest)
                if s := it(6):
                    add_o(s)
                if (s := it(0)) and early:
                    gather(s, 0)
                if s := it(0):
                    gather(s, 1)
                if s := it(6):
                    root(s, var5_ready, 1, rstd5_ready)

            pipeline(pool, LAST, body, count=n)

        @block.sync
        def _(sp):
            def store_v(s):
                sp.wait_ge(v_copied, done(s))
                sp.dma_start(v_d[s.q2], v_new[:, :, :, :].rearrange("p c h e -> p (c h e)")).then_inc(v_there, 16)

            def store_parts(s):
                for a in range(2):
                    sp.wait_ge(split, done(s, 2, a + 1))
                    sp.dma_start(parts_d[a][s.q2].rearrange("j r n -> r j n"), parts[a][:, :, :]).then_inc(parts_there[a][s.q2], 16)

            def load_stacks(s):
                wait_apart(sp, c_set, v_there, done(s) * 16)
                if s.after(4):
                    wait_apart(sp, c_set, products, (s.b - 2 - s.q2) * 32)
                    wait_apart(sp, c_set, weighed, (s.b - 2 - s.q2) * 4)
                sp.dma_start(v[:, s.q4, :, :, :].rearrange("p c h e -> p (c h e)"), v_d[s.q2]).then_inc(stacked[s.q4], 16)
                for a in range(2):
                    wait_apart(sp, c_set, parts_there[a][s.q2], s.b2 * 16 + 16)
                    row = 0
                    for many in range(3, 0, -1):
                        rows = slice(row * DH, (row + many) * DH)
                        if a == 0:
                            sp.dma_start(q_st[rows, s.q4, :, :].rearrange("r h n -> r (h n)"),
                                         parts_d[0][s.q2, 0:many].rearrange("j (d h) n -> (j d) (h n)", h=H)
                                         ).then_inc(stacked[s.q4], 16)
                        else:
                            of_k = parts_d[1][s.q2, 3 - many].rearrange("(d h) n -> d (h n)", h=H)
                            sp.dma_start(k_st[rows, s.q4, :, :].rearrange("r h n -> r (h n)"),
                                         of_k.unsqueeze(0).to_broadcast([many, DH, H * L])).then_inc(stacked[s.q4], 16)
                        row += many

            def store_res(s):
                sp.wait_ge(res_ready, done(s))
                sp.dma_start(out[bass.ds(s.b2 + s.q2 * (B // 2), 1), :, :].rearrange("b (c p) d -> p (b c) d", p=T),
                             res[:, :, :]).then_inc(res_there, 16)

            def body(it):
                if s := it(2):
                    store_v(s)
                if (s := it(3)) and s.q2 == 0:
                    load_stacks(s)
                if s := it(2):
                    store_parts(s)
                if (s := it(2)) and s.q2 == 1:
                    load_stacks(s)
                if s := it(7):
                    store_res(s)

            pipeline(sp, LAST, body)
            sp.wait_ge(res_there, 16 * B)

        @block.tensor
        def _(pe):
            class Misc:
                last = None

            def take_misc(it, lag, reader, per=1, of=0):
                if Misc.last:
                    at, was_lag, was_reader, was_per, was_of = Misc.last
                    back = 0 if at is it else 1
                    s = Step(it.i - back - was_lag, it.reg)
                    pe.wait_ge(was_reader, done(s, was_per, was_of))
                Misc.last = (it, lag, reader, per, of)

            def turn_top(it, s, g, lag):
                pe.wait_ge(top_split, done(s, GROUPS, g + 1))
                take_misc(it, lag, top_copied, GROUPS, g + 1)
                for c in range(C):
                    last = pe.matmul(misc[:12, c * T:(c + 1) * T], top_parts[:, g, c, :, :].rearrange("p j h -> p (j h)"),
                                     identb[:, :], start=True, stop=True)
                last.then_inc(top_turned, 1)

            def turn_o(it, s, g, lag):
                pe.wait_ge(o_copied, done(s, GROUPS, g + 1))
                take_misc(it, lag, o_normed, GROUPS, g + 1)
                for c in range(C):
                    last = pe.transpose(misc[:T, c * 128:(c + 1) * 128], o_t[:, c * T:(c + 1) * T], ident[:, :])
                last.then_inc(o_turned, 1)

            def turn_x4(it, s, lag):
                pe.wait_ge(x4_ready, done(s))
                take_misc(it, lag, x4t_copied)
                for c in range(C):
                    last = pe.transpose(misc[:, c * T:(c + 1) * T], x4[:, c, :], ident[:T, :T])
                last.then_inc(x4t_ready, 1)

            def project_v(it, s, lag):
                pe.wait_ge(x4t_copied, done(s))
                take_misc(it, lag, v_copied)
                for c in range(C):
                    last = pe.matmul(misc[:T, c * D:(c + 1) * D], x4_t[:, c * T:(c + 1) * T], w_t[:, 5, :],
                                     start=True, stop=True)
                last.then_inc(v_ready, 1)

            def project(it, s, a, lag):
                take_misc(it, lag, (q_rest, k_rest)[a])
                pe.matmul(misc[:, :L], qk_w[:, a, :], x4_t[:, :],
                          start=True, stop=True).then_inc((q_ready, k_ready)[a], 1)

            def score(s, t, k):
                head, c = t // 2, t % 2 * 2 + k
                if t == 0 and k == 0:
                    pe.wait_ge(stacked[s.q4], s.b4 * 112 + 112)
                    pe.wait_ge(stacked[s.q4 ^ 1], s.b4 * 112 + 112)
                if k == 0 and (t >= 2 or s.after(1)):
                    pe.wait_ge(reduced, s.b * 16 + t - 1)
                last = pe.matmul(max_ps[:T, t % 2, k, :L], q_st[:NROW, s.q4, head, c * T:(c + 1) * T],
                                 k_st[:NROW, s.q4 ^ 1, head, :], start=True, stop=True)
                if k == 1:
                    last.then_inc(scored, 1)

            def product(s, t, k):
                unit, head = t // 4, t // 8 * 4 + t % 4
                c = unit % 2 * 2 + k
                if t % 8 == 0 and k == 0:
                    pe.wait_ge(top_there[t // 8], done(s) * 16)
                if t >= 1 or s.after(1):
                    pe.wait_ge(exps, s.b * 32 + 2 * t + k - 1)
                pe.matmul(s_ps[:T, k, :L], k_st[:, s.q4 ^ 1, head, c * T:(c + 1) * T], q_st[:, s.q4, head, :],
                          start=True, stop=True).then_inc(products, 1)

            def weigh(s, unit, k):
                if k == 0:
                    pe.wait_ge(exps, s.b * 32 + 8 * unit + 8)
                    if unit % 2 == 0:
                        if unit == 0:
                            if s.after(1):
                                pe.wait_ge(o_copied, s.b * 2)
                        else:
                            pe.wait_ge(o_copied, s.b * 2 + 1)
                c = unit % 2 * 2 + k
                for j in range(4):
                    head = unit // 2 * 4 + j
                    last = pe.matmul(o_ps[32 * j:32 * j + DH + 1, :L], v[:, s.q4 ^ 1, c, head, :], p[:, unit % 2, j, k, :],
                                     start=c == 0, stop=c == 3, skip_group_check=True)
                if k == 1:
                    last.then_inc(weighed, 1)

            def body(it):
                maxima, before, now = it(4), it(6), it(5)
                for t in range(16):
                    for k in range(2):
                        if now:
                            product(now, t, k)
                        if maxima:
                            score(maxima, t, k)
                    if t % 2:
                        if t < 4:
                            if before:
                                weigh(before, 3, t % 4 // 2)
                        elif now:
                            weigh(now, t // 4 - 1, t % 4 // 2)
                    if t == 0 and before:
                        turn_o(it, before, 0, 6)
                    if t == 2 and now:
                        turn_top(it, now, 1, 5)
                    if t == 4 and (s := it(2)):
                        project(it, s, 0, 2)
                    if t == 6 and (s := it(2)):
                        project(it, s, 1, 2)
                    if t == 8 and before:
                        turn_o(it, before, 1, 6)
                    if t == 10 and maxima:
                        turn_top(it, maxima, 0, 4)
                    if t == 12 and (s := it(1)):
                        turn_x4(it, s, 1)
                    if t == 14 and (s := it(1)):
                        project_v(it, s, 1)

            pipeline(pe, LAST, body)

        @block.scalar
        def _(act):
            def exponentials(now, t):
                if t % 4 == 0 and (t >= 8 or now.after(1)):
                    act.wait_ge(weighed, now.b * 4 + t // 4 - 1)
                for k in range(2):
                    act.wait_ge(products, now.b * 32 + 2 * t + k + 1)
                    act.activation(p[:, t // 4 % 2, t % 4, k, :], s_ps[:T, k, :L], ACT.Exp,
                                   scale=float(D) ** -0.5).then_inc(exps, 1)

            def copy_top(s, g):
                act.wait_ge(top_turned, done(s, GROUPS, g + 1))
                if g or s.after(1):
                    act.wait_ge(top_stored, s.b * 32 + 16 * g)
                act.copy(top_rows[:, :], misc[:12, :L]).then_inc(top_copied, 1)

            def store_top(s, g):
                act.wait_ge(top_copied, done(s, GROUPS, g + 1))
                act.dma_start(top_d[g, :, :], top_rows[:, :]).then_inc(top_stored, 16)

            def load_top(s, g):
                act.wait_ge(top_stored, s.b * 32 + 16 * (g + 1))
                act.dma_start(q_st[NROW:SROW, s.q4, 4 * g:4 * g + 4, :].rearrange("j h n -> j (h n)"),
                              top_d[g, :, :].rearrange("(j h) n -> j (h n)", j=3)).then_inc(top_there[g], 16)

            def copy_o(s, g):
                act.wait_ge(weighed, s.b * 4 + 2 * g + 2)
                if g or s.after(1):
                    act.wait_ge(o_turned, s.b * 2 + g)
                act.copy(o_t[:, :], o_ps[:, :L]).then_inc(o_copied, 1)

            def scale_second(s, chunks):
                wait_apart(act, c_set, y_there[s.q2], s.b2 * 128 + 128)
                for c in chunks:
                    last = act.activation(y[:, s.q2, 2 * c + 1, :], y[:, s.q2, 2 * c + 1, :], ACT.Copy,
                                          scale=share[:, bass.ds(tile(s) + c, 1), 1:2].rearrange("p a k -> p (a k)"))
                if C - 1 in chunks:
                    last.then_inc(second_scaled, 1)

            def norm(s, norm, dest, scale, chunks, ready):
                for c in chunks:
                    last = act.activation(dest[:, c, :], h[:, bass.ds(tile(s) + c, 1), :].rearrange("p a d -> p (a d)"),
                                          ACT.Identity, bias=c_shift[:, norm, c:c + 1], scale=scale[:, c:c + 1])
                if C - 1 in chunks:
                    last.then_inc(ready, 1)

            def copy_first(s, a):
                act.wait_ge((q_ready, k_ready)[a], done(s))
                if s.after(1):
                    act.wait_ge(parts_there[a][1 - s.q2], s.b2 * 16 + (16 if s.q2 else 0))
                act.copy(parts[a][:, 0, :], misc[:, :L]).then_inc((q1_copied, k1_copied)[a], 1)

            def body(it):
                summed, projected, maxima, now, before, past = it(1), it(2), it(4), it(5), it(6), it(7)
                for t in range(16):
                    if t == 13 and summed:
                        act.wait_ge(x4t_ready, done(summed))
                        if summed.after(1):
                            act.wait_ge(k_ready, summed.b)
                        act.copy(x4_t[:, :], misc[:, :L]).then_inc(x4t_copied, 1)
                    if t == 5 and projected:
                        copy_first(projected, 0)
                    if t == 7 and projected:
                        copy_first(projected, 1)
                    if now:
                        exponentials(now, t)
                    if t < 2 and summed:
                        scale_second(summed, (2 * t, 2 * t + 1))
                    if t in (6, 8) and past:
                        if t == 6:
                            wait_apart(act, c_set, gain_ready, done(past))
                            if past.after(1):
                                wait_apart(act, c_set, res_there, past.b * 16)
                        norm(past, 1, res, c_gain, (0, 1) if t == 6 else (2, 3), res_ready)
                    if t == 3 and now:
                        copy_top(now, 1)
                        store_top(now, 1)
                    if t == 5 and now:
                        load_top(now, 1)
                    if t == 4 and before:
                        copy_o(before, 1)
                    if t in (9, 10) and summed:
                        if t == 9:
                            wait_apart(act, c_set, shift4_ready, done(summed))
                            if summed.after(1):
                                wait_apart(act, c_set, x4t_ready, summed.b)
                        norm(summed, 0, x4, c_rstd[:, 0, :], (2 * t - 18, 2 * t - 17), x4_ready)
                    if t == 11 and maxima:
                        copy_top(maxima, 0)
                        store_top(maxima, 0)
                    if t == 13 and maxima:
                        load_top(maxima, 0)
                    if t == 12 and now:
                        copy_o(now, 0)
                    if t == 15 and summed:
                        act.wait_ge(v_ready, done(summed))
                        if summed.after(1):
                            act.wait_ge(v_there, summed.b * 16)
                        act.copy(v_new[:, :, :, 0:DH], misc[:T, :].rearrange("p (c h d) -> p c h d", c=C, h=H)
                                 ).then_inc(v_copied, 1)

            pipeline(act, LAST, body)

        @block.vector
        def _(dve):
            n = Count(vec_done)
            n.n = vec_from.n

            def maximum(s, t):
                dve.wait_ge(scored, s.b * 16 + t + 1)
                if t % 8 == 0 and s.after(1):
                    dve.wait_ge(top_split, done(s, GROUPS, t // 8 + 1) - 2)
                dve.tensor_reduce(top[:, t // 8, t // 2 % 4, t % 2 * 2:t % 2 * 2 + 2], max_ps[:T, t % 2, :, :L], axis=AX.X,
                                  op=ALU.max, negate=True).then_inc(reduced, 1)

            def split_top(s, g):
                dve.wait_ge(reduced, s.b * 16 + 8 * g + 8)
                if s.after(1):
                    dve.wait_ge(top_turned, done(s, GROUPS, g + 1) - 2)
                by_head = top_parts[:, g, :, :, :].rearrange("p c j h -> p j h c")
                got = n.done(dve.tensor_copy(by_head[:, 0, :, :], top[:, g, :, :]))
                dve.wait_ge(vec_done, got)
                got = n.done(dve.tensor_tensor(top_rest[:, :, :], top[:, g, :, :], by_head[:, 0, :, :], ALU.subtract))
                dve.wait_ge(vec_done, got)
                got = n.done(dve.tensor_copy(by_head[:, 1, :, :], top_rest[:, :, :]))
                dve.wait_ge(vec_done, got)
                dve.tensor_tensor(by_head[:, 2, :, :], top_rest[:, :, :], by_head[:, 1, :, :], ALU.subtract).then_inc(top_split, 1)

            def add_first(s, chunks):
                if 0 in chunks:
                    dve.wait_ge(y_there[s.q2], s.b2 * 128 + 128)
                for c in chunks:
                    here = h[:, bass.ds(tile(s) + c, 1), :].rearrange("p a d -> p (a d)")
                    last = dve.scalar_tensor_tensor(
                        out=here, in0=y[:, s.q2, 2 * c, :], scalar=share[:, bass.ds(tile(s) + c, 1), 0:1],
                        in1=here, op0=ALU.mult, op1=ALU.add)
                if C - 1 in chunks:
                    last.then_inc(first_added, 1)

            def stats_of(s, norm, chunks):
                for c in chunks:
                    taken = n.done(dve.bn_stats(c_stats[:, norm, c, :], h[:, bass.ds(tile(s) + c, 1), :]))
                return taken

            def moments_of(s, norm, taken):
                for c in range(C):
                    if c == 0:
                        wait_apart(dve, c_set, vec_done, taken)
                    got = n.done(dve.bn_aggr(c_mom[:, s.q2, norm, c, :], c_stats[:, norm, c, :]))
                dve.wait_ge(vec_done, got)

            def variance(s, norm, ready):
                dve.tensor_scalar(c_var[:, norm, :], c_mom[:, s.q2, norm, :, 1], EPS, None, ALU.add).then_inc(ready, 1)

            def norm_o(s, g):
                dve.wait_ge(o_turned, done(s, GROUPS, g + 1))
                turned = misc[:T, :].rearrange("p (c h e) -> p c h e", c=C, h=4)
                got = n.done(dve.reciprocal(o_inv[:, :, :], turned[:, :, :, DH]))
                dve.wait_ge(vec_done, got)
                if g == 0 and s.after(2):
                    dve.wait_ge(h_done, s.b - 1)
                dve.tensor_tensor(o[:, s.q2, :, :].rearrange("p c (d h) -> p c h d", h=H)[:, :, 4 * g:4 * g + 4, :],
                                  turned[:, :, :, 0:DH], bc(o_inv[:, :, :], 3, DH, [T, C, 4, DH]), ALU.mult).then_inc(o_normed, 1)

            def rest_of(s, a):
                dve.wait_ge((q1_copied, k1_copied)[a], done(s))
                if a or s.after(1):
                    dve.wait_ge(split, s.b * 2 + a)
                dve.tensor_tensor(rest[:, :], misc[:, :L], parts[a][:, 0, :], ALU.subtract).then_inc((q_rest, k_rest)[a], 1)

            def body(it):
                summed, projected, maxima, now, before = it(1), it(2), it(4), it(5), it(6)
                for t in range(16):
                    if t == 0 and now:
                        split_top(now, 1)
                    if t in (1, 9) and before:
                        norm_o(before, t // 8)
                    if t in (5, 7) and projected:
                        rest_of(projected, t // 7)
                    if maxima:
                        maximum(maxima, t)
                    if summed:
                        if t == 1:
                            add_first(summed, (0, 1))
                        if t == 2:
                            add_first(summed, (2, 3))
                        if t == 4:
                            wait_apart(dve, c_set, combined, done(summed))
                            stats_of(summed, 0, (0, 1))
                        if t == 6:
                            taken = stats_of(summed, 0, (2, 3))
                            moments_of(summed, 0, taken)
                            if summed.after(1):
                                dve.wait_ge(rstd4_ready, summed.b)
                            variance(summed, 0, var4_ready)
                        if t == 8:
                            dve.wait_ge(rstd4_ready, done(summed))
                            if summed.after(1):
                                dve.wait_ge(x4_ready, summed.b)
                            dve.scalar_tensor_tensor(out=c_shift[:, 0, :], in0=c_mom[:, summed.q2, 0, :, 0], scalar=-1.0,
                                                     in1=c_rstd[:, 0, :], op0=ALU.mult, op1=ALU.mult).then_inc(shift4_ready, 1)
                    if t == 8 and maxima:
                        split_top(maxima, 0)
                    if before:
                        if t == 11:
                            wait_apart(dve, c_set, h_done, done(before))
                            stats_of(before, 1, (0, 1))
                        if t == 12:
                            taken5 = stats_of(before, 1, (2, 3))
                        if t == 13:
                            moments_of(before, 1, taken5)
                            if before.after(1):
                                dve.wait_ge(rstd5_ready, before.b)
                            variance(before, 1, var5_ready)
                        if t == 14:
                            dve.wait_ge(rstd5_ready, done(before))
                            if before.after(1):
                                dve.wait_ge(res_ready, before.b)
                            n.done(dve.tensor_scalar(c_gain[:, :], c_rstd[:, 1, :], 1.0, None, ALU.add))
                            got = n.now()
                            dve.wait_ge(vec_done, got)
                            dve.scalar_tensor_tensor(out=c_shift[:, 1, :], in0=c_mom[:, before.q2, 1, :, 0], scalar=-1.0,
                                                     in1=c_rstd[:, 1, :], op0=ALU.mult, op1=ALU.mult).then_inc(gain_ready, 1)

            pipeline(dve, LAST, body, count=n)


_INS = ['x', 'fside_BS_value', 'L0_tok_emb_table', 'L0_tok_w_val', 'L0_tok_b_val', 'L0_tok_gamma_g', 'L0_tok_beta_g',
        'L0_tok_gamma_v', 'L0_tok_beta_v', 'L0_attn_Wg', 'L0_attn_bg', 'L0_attn_Wc', 'L0_attn_bc', 'L0_ffn_gate_w',
        'L0_ffn_w1', 'L0_ffn_w3', 'L0_ffn_w2', 'L0_ffn_sw1', 'L0_ffn_sw3', 'L0_ffn_sw2', 'L1_attn_q_w', 'L1_attn_kv_w']


def kernel(**inputs):
    import numpy as np
    from concourse import bacc
    from concourse.bass_utils import run_bass_kernel_spmd

    nc = bacc.Bacc("TRN2", target_bir_lowering=False, num_devices=1)
    arrays, io = {}, {}
    for name in _INS:
        arrays["in_" + name] = np.ascontiguousarray(inputs[name])
        a = arrays["in_" + name]
        io[name] = nc.dram_tensor("in_" + name, a.shape, mybir.dt.from_np(a.dtype), kind="ExternalInput").ap()
    out = nc.dram_tensor("out_h", (B, L, D), F32, kind="ExternalOutput").ap()
    build(nc, io, out)
    return run_bass_kernel_spmd(nc, [arrays], core_ids=[0]).results[0]["out_h"]
```
